# Optimizing a Trainium2 kernel written in Bass

```python
import numpy as np
import jax
import jax.numpy as jnp

def _softmax(x, axis=-1):
    return jax.nn.softmax(x, axis=axis)

def _gelu(x):
    return jax.nn.gelu(x, approximate=True)

def _silu(x):
    return jax.nn.silu(x)

def _sigmoid(x):
    return jax.nn.sigmoid(x)

def _layernorm(x, axis=-1, eps=1e-05):
    m = jnp.mean(x, axis=axis, keepdims=True)
    v = jnp.var(x, axis=axis, keepdims=True)
    return (x - m) / jnp.sqrt(v + eps)

def _scatter_add(tgt, idx, src, axis=0):
    return tgt.at[idx].add(src)

def _segment_sum(src, seg, n):
    return jax.ops.segment_sum(src, seg, n)
kernel_name = 'mk_vit_tower_d1_tok_img768_r4_7ef2d5'

def setup_inputs(seed: int=0):
    np.random.seed(seed)
    _w = jnp.asarray

    def _rec_inputs():
        import jax
        import jax.numpy as jnp
        _rk = jax.random.key(seed)
        x = -0.00016672 + 0.999947 * jax.random.normal(jax.random.fold_in(_rk, 1), (64, 224, 224, 3), jnp.float32)
        return x
    x = _rec_inputs()

    def _L0_tok_setup():
        import jax, jax.numpy as jnp
        import numpy as np
        PATCH = 16
        EMBED = 192
        key = jax.random.key(seed)
        k1, k2 = jax.random.split(key)
        images = jax.random.normal(k1, (64, 96, 96, 3), dtype=jnp.float32)
        patch_dim = PATCH * PATCH * 3
        W = jax.random.normal(k2, (patch_dim, EMBED), dtype=jnp.float32) * patch_dim ** (-0.5)
        b = jnp.zeros((EMBED,), dtype=jnp.float32)
        return {'images': images, 'W': W, 'b': b}
    _L0_tok_all = _L0_tok_setup()
    _L0_tok_in = {k: v for k, v in _L0_tok_all.items() if k in ('W', 'b')}
    del _L0_tok_all

    def _L0_attn_setup():
        import jax, jax.numpy as jnp
        import numpy as np
        DIM = 192
        NUM_HEADS = 12
        HEAD_DIM = DIM // NUM_HEADS
        key = jax.random.key(seed)
        k_x, k_a, k_v, k_p, k_b = jax.random.split(key, 5)
        B, N = (4, 512)
        s = 0.02
        return {'x': jax.random.normal(k_x, (B, N, DIM), dtype=jnp.float32), 'W_A': jax.random.normal(k_a, (DIM, NUM_HEADS), dtype=jnp.float32) * s, 'W_V': jax.random.normal(k_v, (DIM, DIM), dtype=jnp.float32) * s, 'W_proj': jax.random.normal(k_p, (DIM, DIM), dtype=jnp.float32) * s, 'b_proj': jax.random.normal(k_b, (DIM,), dtype=jnp.float32) * s}
    _L0_attn_all = _L0_attn_setup()
    _L0_attn_in = {k: v for k, v in _L0_attn_all.items() if k in ('W_A', 'W_V', 'W_proj', 'b_proj')}
    del _L0_attn_all

    def _L0_ffn_setup():
        import jax, jax.numpy as jnp
        import numpy as np
        EPS = 1e-06

        def l2_normalize(x, axis):
            norm = jnp.sqrt(jnp.square(x).sum(axis=axis, keepdims=True))
            return x * (1.0 / (norm + EPS))
        key = jax.random.key(seed)
        ks = jax.random.split(key, 8)
        b, m, d = (32, 256, 192)
        n, p = (8, 4)
        h = d // 8
        X = jax.random.normal(ks[0], (b, m, d), dtype=jnp.float32)
        std_slot = float(np.sqrt(2.0 / (d + n * p)))
        slot_params = jax.random.normal(ks[1], (d, n, p), dtype=jnp.float32) * std_slot
        scale = jnp.ones((), dtype=jnp.float32)
        W_down = jax.random.normal(ks[2], (n, d, h), dtype=jnp.float32) * float(np.sqrt(1.0 / d))
        b_down = jnp.zeros((n, h), dtype=jnp.float32)
        W_up = jax.random.normal(ks[3], (n, h, d), dtype=jnp.float32) * float(np.sqrt(1.0 / h))
        b_up = jnp.zeros((n, d), dtype=jnp.float32)
        return {'X': X, 'slot_params': slot_params, 'scale': scale, 'W_down': W_down, 'b_down': b_down, 'W_up': W_up, 'b_up': b_up}
    _L0_ffn_all = _L0_ffn_setup()
    _L0_ffn_in = {k: v for k, v in _L0_ffn_all.items() if k in ('slot_params', 'scale', 'W_down', 'b_down', 'W_up', 'b_up')}
    del _L0_ffn_all
    return {'x': x, 'L0_tok_W': _L0_tok_in['W'], 'L0_tok_b': _L0_tok_in['b'], 'L0_attn_W_A': _L0_attn_in['W_A'], 'L0_attn_W_V': _L0_attn_in['W_V'], 'L0_attn_W_proj': _L0_attn_in['W_proj'], 'L0_attn_b_proj': _L0_attn_in['b_proj'], 'L0_ffn_slot_params': _L0_ffn_in['slot_params'], 'L0_ffn_scale': _L0_ffn_in['scale'], 'L0_ffn_W_down': _L0_ffn_in['W_down'], 'L0_ffn_b_down': _L0_ffn_in['b_down'], 'L0_ffn_W_up': _L0_ffn_in['W_up'], 'L0_ffn_b_up': _L0_ffn_in['b_up']}

def reference(x, L0_tok_W, L0_tok_b, L0_attn_W_A, L0_attn_W_V, L0_attn_W_proj, L0_attn_b_proj, L0_ffn_slot_params, L0_ffn_scale, L0_ffn_W_down, L0_ffn_b_down, L0_ffn_W_up, L0_ffn_b_up):
    import jax
    import jax.numpy as jnp

    def _L0_tok_ref(images, W, b):
        import jax, jax.numpy as jnp
        import numpy as np
        PATCH = 16
        EMBED = 192
        B, H, Wd, C = images.shape
        p = PATCH
        hp, wp = (H // p, Wd // p)
        x = images.reshape(B, hp, p, wp, p, C)
        x = x.transpose(0, 1, 3, 2, 4, 5)
        x = x.reshape(B, hp * wp, p * p * C)
        return jnp.einsum('bnd,de->bne', x, W) + b

    def _L0_attn_ref(x, W_A, W_V, W_proj, b_proj):
        import jax, jax.numpy as jnp
        import numpy as np
        DIM = 192
        NUM_HEADS = 12
        HEAD_DIM = DIM // NUM_HEADS
        B, N, C = x.shape
        h, hd = (NUM_HEADS, HEAD_DIM)
        z = jnp.einsum('bnc,ch->bhn', x, W_A)
        z_star = jax.nn.softmax(z, axis=-1)
        pos = jnp.arange(N)
        idx = (pos[None, :] - pos[:, None]) % N
        roll = z_star[:, :, idx] / N
        V = jnp.einsum('bnc,cd->bnd', x, W_V).reshape(B, N, h, hd).transpose(0, 2, 1, 3)
        out = jnp.einsum('bhij,bhjd->bhid', roll, V)
        out = out.transpose(0, 2, 1, 3).reshape(B, N, C)
        out = jnp.einsum('bnc,cd->bnd', out, W_proj) + b_proj
        return out

    def _L0_ffn_ref(X, slot_params, scale, W_down, b_down, W_up, b_up):
        import jax, jax.numpy as jnp
        import numpy as np
        EPS = 1e-06

        def l2_normalize(x, axis):
            norm = jnp.sqrt(jnp.square(x).sum(axis=axis, keepdims=True))
            return x * (1.0 / (norm + EPS))
        b, m, d = X.shape
        _, n, p = slot_params.shape
        Xn = l2_normalize(X, axis=-1)
        sp = l2_normalize(slot_params, axis=1) * scale
        logits = jnp.einsum('bmd,dnp->bmnp', Xn, sp)
        D = jax.nn.softmax(logits, axis=1)
        C = jax.nn.softmax(logits.reshape(b, m, n * p), axis=2).reshape(b, m, n, p)
        X_tilde = jnp.einsum('bmd,bmnp->bnpd', Xn, D)
        H = jax.nn.gelu(jnp.einsum('bnpd,ndh->bnph', X_tilde, W_down) + b_down[None, :, None, :], approximate=False)
        Y_tilde = jnp.einsum('bnph,nhd->bnpd', H, W_up) + b_up[None, :, None, :]
        Y = jnp.einsum('bnpd,bmnp->bmd', Y_tilde, C)
        return Y
    h = _L0_tok_ref(x, L0_tok_W, L0_tok_b)
    h = h + _L0_attn_ref(_layernorm(h, axis=-1), L0_attn_W_A, L0_attn_W_V, L0_attn_W_proj, L0_attn_b_proj)
    h = h + _L0_ffn_ref(_layernorm(h, axis=-1), L0_ffn_slot_params, L0_ffn_scale, L0_ffn_W_down, L0_ffn_b_down, L0_ffn_W_up, L0_ffn_b_up)
    return h

_drawn_inputs = setup_inputs


def setup_inputs(seed=0):
    import zlib

    import numpy as np

    out = dict(_drawn_inputs(seed))
    spreads = {'L0_tok_b': (0.0, 0.1), 'L0_ffn_b_down': (0.0, 0.421), 'L0_ffn_b_up': (0.0, 0.301)}
    factors = {'L0_attn_W_A': 54.408,
     'L0_attn_W_V': 51.064,
     'L0_attn_W_proj': 51.713,
     'L0_attn_b_proj': 2.949,
     'L0_ffn_slot_params': 8.0,
     'L0_ffn_W_down': 8.0,
     'L0_ffn_W_up': 3.023}
    for name, (base, spread) in spreads.items():
        noise = np.random.default_rng([zlib.crc32(name.encode()), seed]).standard_normal(out[name].shape)
        drawn = base * np.exp(spread * noise) if base else spread * noise
        out[name] = jnp.asarray(drawn.astype(out[name].dtype))
    for name, factor in factors.items():
        out[name] = (out[name] * factor).astype(out[name].dtype)
    return out
```

```python
import numpy as np
from contextlib import ExitStack

import concourse.bass as bass
from concourse import mybir
from concourse.alu_op_type import AluOpType as ALU

F32 = mybir.dt.float32
ACT = mybir.ActivationFunctionType
AX = mybir.AxisListType

IMAGES, SIDE, PATCH, COLORS = 64, 224, 16, 3
GRID = SIDE // PATCH
TOK = GRID * GRID
HALF = TOK // 2
QTR = HALF // 2
DIM = 192
CH = DIM // 2
PIX = PATCH * COLORS
PDIM = PATCH * PIX
KQ = PDIM // 128
HEADS = 12
HD = DIM // HEADS
GI = 8
GROUPS = IMAGES // GI
GROWS = GI * GRID
QI = 4
NE, NP = 8, 4
SLOTS = NE * NP
HID = DIM // 8
J_ACT = 4
J_VEC = GRID - J_ACT
LN_EPS, L2_EPS = 1e-5, 1e-6
VECTOR_LINKS = 33


def tables():
    j = np.arange(HALF)[:, None]
    k_even, k_odd = 2 * np.arange(QTR), 2 * np.arange(QTR) + 1

    def cos_sin(tokens, cos_k, sin_k):
        w = 2 * np.pi / TOK
        return np.cos(w * tokens * cos_k), np.sin(w * tokens * sin_k)

    k = np.concatenate([k_even, k_odd])
    even_c, even_s = cos_sin(j, k_even[None], k_even[None])
    even_s[:, 0] = (-1.0) ** j[:, 0]
    odd_c, odd_s = cos_sin(j, k_odd[None], k_odd[None])
    forward = np.stack([np.concatenate([even_c, even_s], 1), np.concatenate([odd_c, odd_s], 1)], 1)
    t = np.arange(TOK)
    inv_c, inv_s = cos_sin(t[None], k[:, None], k[:, None])
    weight = np.where(k == 0, 1.0, 2.0)[:, None] / TOK
    inv_c, inv_s = inv_c * weight, inv_s * weight
    inv_s[0] = (-1.0) ** t / TOK
    inverse = np.stack([inv_c, inv_s], 1)
    all_c, all_s = cos_sin(t[:, None], k[None], k[None])
    own_s = all_c.copy()
    own_s[:, 0] = (-1.0) ** t
    heads = np.stack([all_c, own_s, -all_s], 1) / TOK
    heads = heads.reshape(2, HALF, 3, HALF).transpose(1, 0, 2, 3)
    mask = np.zeros((128, 2, NE, NP))
    one = np.zeros((128, 1))
    for n in range(NE):
        mask[32 * (n % 4):32 * (n % 4) + HID + 1, n // 4, n, :] = 1.0
        one[32 * (n % 4) + HID] = 1.0
    out = {"ident": np.eye(128), "forward": forward, "inverse": inverse, "heads": heads,
           "mask": mask.reshape(128, 2, SLOTS), "one": one}
    return {n: np.ascontiguousarray(a, dtype=np.float32) for n, a in out.items()}


def build(nc, x, tok_W, tok_b, W_A, W_V, W_proj, b_proj, slot_params, scale, W_down, b_down, W_up,
          b_up, t_ident, t_forward, t_inverse, t_heads, t_mask, t_one, out):
    ctx = ExitStack()
    with ctx:
        def sb(name, shape):
            return ctx.enter_context(nc.sbuf_tensor(name, shape, F32))

        def sem(name):
            return ctx.enter_context(nc.semaphore(name))

        ident = sb("ident", [128, 128])
        fwd = sb("fwd", [HALF, 2, HALF])
        inv = sb("inv", [HALF, 2, TOK])
        headb = sb("headb", [HALF, 2, 3, HALF])
        mask = sb("mask", [128, 2, SLOTS])
        one = sb("one", [128, 1])
        w_tok = sb("w_tok", [128, KQ, DIM])
        b_tok = sb("b_tok", [GROWS, DIM])
        w_a = sb("w_a", [CH, 2, 32])
        w_v = sb("w_v", [CH, 2, DIM])
        w_p = sb("w_p", [CH + 1, 2, DIM])
        slots = sb("slots", [CH, 2, SLOTS])
        slots_sq = sb("slots_sq", [CH, 2, SLOTS])
        slot_norm = sb("slot_norm", [CH, 4, 2, NP])
        slots_n = sb("slots_n", [CH, 2, SLOTS])
        scale_c = sb("scale_c", [CH, 1])
        halves = sb("halves", [128, 2, GI])
        neg_halves = sb("neg_halves", [128, 2, GI])
        w_dn = sb("w_dn", [CH, 2, NE, 32])
        w_up = sb("w_up", [128, 2, DIM])
        b_dn = sb("b_dn", [128, 2])

        x_raw = [sb(f"x_raw{i}", [GROWS, PATCH, GRID // 2 * PIX]) for i in range(2)]
        x_pat = [sb(f"x_pat{i}", [GROWS, PDIM]) for i in range(2)]
        x_t = [sb(f"x_t{i}", [128, KQ, GROWS]) for i in range(2)]
        h_rows = sb("h_rows", [GROWS, GRID, DIM])
        h = sb("h", [HALF, 2, GI, DIM])
        h1 = sb("h1", [HALF, 2, GI, DIM])
        st = sb("st", [HALF, 2, GI, 6])
        sm = sb("sm", [HALF, 8, 2, GI])
        xln = [sb(f"xln{i}", [HALF, 2, DIM]) for i in range(4)]
        sumdif = [sb(f"sumdif{i}", [HALF, 2, DIM]) for i in range(4)]
        spec = [sb(f"spec{i}", [CH, 2, TOK]) for i in range(GI)]
        zh = [sb(f"zh{i}", [128, TOK]) for i in range(2)]
        zh_t = [sb(f"zh_t{i}", [HALF, 2, 128]) for i in range(2)]
        z_e = [sb(f"z_e{i}", [128, TOK]) for i in range(2)]
        z_n = [sb(f"z_n{i}", [128, TOK]) for i in range(2)]
        z_m = sb("z_m", [128, 2, 3])
        z_t = [sb(f"z_t{i}", [HALF, 2, 128]) for i in range(2)]
        coef = [sb(f"coef{i}", [HALF, 4, QI, HEADS]) for i in range(2)]
        v_own = [sb(f"v_own{i}", [HALF, 2, DIM]) for i in range(2)]
        v_cross = [sb(f"v_cross{i}", [HALF, 2, DIM]) for i in range(2)]
        u_spec = [sb(f"u_spec{i}", [HALF, 2, DIM]) for i in range(2)]
        mix_t = [sb(f"mix_t{i}", [CH + 1, 2, TOK]) for i in range(2)]
        xn = sb("xn", [HALF, GI, 2, DIM])
        xn_t = [sb(f"xn_t{i}", [CH, 2, TOK]) for i in range(2)]
        lg = [sb(f"lg{i}", [128, TOK]) for i in range(2)]
        d_e = [sb(f"d_e{i}", [128, TOK]) for i in range(2)]
        d_m = sb("d_m", [128, 2, 3])
        d_t = [sb(f"d_t{i}", [HALF, 2, 128]) for i in range(2)]
        c_s = [sb(f"c_s{i}", [HALF, 2 * QI, SLOTS]) for i in range(2)]
        c_e = [sb(f"c_e{i}", [HALF, 2 * QI, SLOTS]) for i in range(2)]
        c_n = [sb(f"c_n{i}", [HALF, 2 * QI, SLOTS]) for i in range(2)]
        c_m = sb("c_m", [HALF, 2, 3, 2 * QI])
        c_t = [sb(f"c_t{i}", [128, 2, HALF]) for i in range(2)]
        xs = [sb(f"xs{i}", [128, DIM]) for i in range(2)]
        xs_t = sb("xs_t", [CH, 2, GI, NE, NP])
        hid = sb("hid", [128, 2, GI * NP])
        hid1 = sb("hid1", [128, 2, GI * NP])
        hid_blk = sb("hid_blk", [128, 2, GI, NE, NP])
        y_blk = [sb(f"y_blk{i}", [128, QI, DIM]) for i in range(2)]
        o_sb = [sb(f"o_sb{i}", [HALF, 2, QI, DIM]) for i in range(2)]

        bank = [ctx.enter_context(nc.psum_tensor(f"bank{i}", [128, 512], F32)) for i in range(8)]
        TR, HB, P = bank[0:2], bank[2:4], bank[4:8]

        s_embed = sem("s_embed")
        s_const = sem("s_const")
        s_zero = sem("s_zero")
        s_pool = sem("s_pool")
        s_ready = sem("s_ready")
        s_x = [sem(f"s_x{i}") for i in range(2)]
        s_pat_a = sem("s_pat_a")
        s_pat_v = sem("s_pat_v")
        s_tr = sem("s_tr")
        s_xt = sem("s_xt")
        s_tok = sem("s_tok")
        s_rows = sem("s_rows")
        s_h = [sem(f"s_hq{i}") for i in range(2)]
        s_var = sem("s_var")
        s_rstd = sem("s_rstd")
        s_xln = sem("s_xln")
        s_sd = sem("s_sd")
        s_A = sem("s_A")
        s_spec = sem("s_spec")
        s_zp = sem("s_zp")
        s_za = sem("s_za")
        s_zv = sem("s_zv")
        s_B = sem("s_B")
        s_v = sem("s_v")
        s_u = sem("s_u")
        s_E = sem("s_E")
        s_mix = sem("s_mix")
        s_D = sem("s_D")
        s_h1 = sem("s_h1")
        s_var2 = sem("s_var2")
        s_root = sem("s_root")
        s_xn = sem("s_xn")
        s_X = sem("s_X")
        s_xnt = sem("s_xnt")
        s_L = sem("s_L")
        s_lmax = sem("s_lmax")
        s_la = sem("s_la")
        s_LT = sem("s_LT")
        s_DT = sem("s_DT")
        s_dt = sem("s_dt")
        s_csub = sem("s_csub")
        s_cexp = sem("s_cexp")
        s_cn = sem("s_cn")
        s_CT = sem("s_CT")
        s_ct = sem("s_ct")
        s_XS = sem("s_XS")
        s_xs = sem("s_xs")
        s_XST = sem("s_XST")
        s_xst = sem("s_xst")
        s_DN = sem("s_DN")
        s_gelu = sem("s_gelu")
        s_blk = sem("s_blk")
        s_UP = sem("s_UP")
        s_yb = sem("s_yb")
        s_Y = sem("s_Y")
        s_o = sem("s_o")
        s_out = sem("s_out")
        s_vl = sem("s_vl")

        x_v = x.rearrange("b (i r) (s w) c -> s (b i) r (w c)", r=PATCH, s=2)
        out_v = out.rearrange("(q b) (c p) d -> q p c b d", b=QI, p=HALF)

        first = [
            (ident[:, :], t_ident), (w_tok[:, :, :], tok_W.rearrange("(q p) e -> p q e", p=128)),
            (b_tok[:, :], tok_b.rearrange("(o e) -> o e", o=1).to_broadcast([GROWS, DIM])),
        ]
        consts = [
            (fwd[:, :, :], t_forward), (inv[:, :, :], t_inverse),
            (headb[:, :, :, :], t_heads), (mask[:, :, :], t_mask), (one[:, :], t_one),
            (w_v[:, :, :], W_V.rearrange("(s p) e -> p s e", p=CH)),
            (w_p[0:CH, :, :], W_proj.rearrange("(s p) e -> p s e", p=CH)),
            (w_p[CH:CH + 1, 1, :], b_proj.rearrange("(o e) -> o e", o=1)),
            (slots[:, :, :], slot_params.rearrange("(s p) n m -> p s (n m)", p=CH)),
            (scale_c[:, :], scale.to_broadcast([CH, 1])),
        ]
        padded = [(w_a[:, :, 0:HEADS], W_A.rearrange("(s p) e -> p s e", p=CH))]
        for s in range(2):
            padded.append((w_dn[:, s, :, 0:HID], W_down[:, s * CH:(s + 1) * CH, :].rearrange("n p m -> p n m")))
        for n in range(NE):
            at = 32 * (n % 4)
            padded.append((w_up[at:at + HID, n // 4, :], W_up[n]))
            padded.append((w_up[at + HID:at + HID + 1, n // 4, :], b_up[n:n + 1, :]))
            padded.append((b_dn[at:at + HID, n // 4:n // 4 + 1], b_down[n:n + 1, :].rearrange("o m -> m o")))
        N_CONST = 16 * (len(consts) + len(padded))

        block = ctx.enter_context(nc.Block())

        @block.sync
        def _(sp):
            def held(*values):
                return [v if isinstance(v, int) else sp.snap(v) for v in values]

            def load_x(g):
                first_row, out0, out1 = held(g * GROWS, g * J_VEC - GRID // 2, g * J_VEC)
                for s in range(2):
                    if not isinstance(g, int) or g > 0:
                        sp.wait_ge(s_pat_v, (out0, out1)[s])
                    sp.dma_start(x_raw[s][:, :, :], x_v[s, bass.ds(first_row, GROWS)]).then_inc(s_x[s], 16)

            def move_h(g):
                sp.wait_ge(s_rows, g * GRID + GRID)
                for b in range(GI):
                    for c in range(2):
                        r0 = b * GRID + c * (GRID // 2)
                        sp.dma_start(h[:, c, b, :], h_rows[r0:r0 + GRID // 2, :, :]).then_inc(s_h[b // QI], 16)

            def store(g):
                quad0, quad1, out0, out1 = held(g * 2, g * 2 + 1, g * 8 + 4, g * 8 + 8)
                for q in range(2):
                    sp.wait_ge(s_o, (out0, out1)[q])
                    for c in range(2):
                        sp.dma_start(out_v[bass.ds((quad0, quad1)[q], 1), :, c].rearrange("o p b d -> (o p) b d"),
                                     o_sb[q][:, c, :, :]).then_inc(s_out, 16)

            for dst, src in first[:1]:
                sp.dma_start(dst, src).then_inc(s_embed, 16)
            sp.dma_start(x_raw[0][:, :, :], x_v[0, 0:GROWS]).then_inc(s_x[0], 16)
            for dst, src in first[1:]:
                sp.dma_start(dst, src).then_inc(s_embed, 16)
            sp.dma_start(x_raw[1][:, :, :], x_v[1, 0:GROWS]).then_inc(s_x[1], 16)
            for dst, src in consts:
                sp.dma_start(dst, src).then_inc(s_const, 16)
            sp.wait_ge(s_zero, 1)
            for dst, src in padded:
                sp.dma_start(dst, src).then_inc(s_const, 16)
            sp.sem_inc(s_out, 16)
            load_x(1)
            move_h(0)
            with sp.Fori(0, GROUPS - 2) as g:
                load_x(g + 2)
                move_h(g + 1)
                store(g)
            move_h(GROUPS - 1)
            store(GROUPS - 2)
            store(GROUPS - 1)
            sp.wait_ge(s_out, 16 + GROUPS * 64)

        @block.gpsimd
        def _(pool):
            for t in (w_a, w_dn, w_up, b_dn, y_blk[0], y_blk[1]):
                nc.gpsimd.memset(t[...], 0.0)
            nc.gpsimd.memset(halves[:, :, :], 0.5)
            nc.gpsimd.memset(neg_halves[:, :, :], -0.5).then_inc(s_pool, 1)
            pool.wait_ge(s_pool, 1)
            nc.gpsimd.memset(mix_t[0][CH:CH + 1, :, :], 1.0)
            nc.gpsimd.memset(mix_t[1][CH:CH + 1, :, :], 1.0).then_inc(s_zero, 1)
            pool.wait_ge(s_zero, 1)
            pool.wait_ge(s_ready, 2)
            nc.gpsimd.tensor_tensor(slot_norm[:, 1], slot_norm[:, 0], halves[0:CH, :, 0:NP], ALU.pow).then_inc(s_ready, 1)

            def group(g):
                for q in range(2):
                    b4 = slice(q * QI, q * QI + QI)
                    pool.wait_ge(s_var, g * 2 + q + 1)
                    nc.gpsimd.tensor_tensor(sm[:, 1, :, b4], sm[:, 3, :, b4], neg_halves[0:HALF, :, b4],
                                            ALU.pow).then_inc(s_rstd, 1)
                    for b in range(q * QI, q * QI + QI):
                        pool.wait_ge(s_xln, g * GI + b + 1)
                        if b >= 4:
                            pool.wait_ge(s_A, g * GI + b - 3)
                        a = xln[b % 4]
                        nc.gpsimd.tensor_tensor(sumdif[b % 4][:, 0, :], a[:, 0, :], a[:, 1, :], ALU.add)
                        nc.gpsimd.tensor_tensor(sumdif[b % 4][:, 1, :], a[:, 0, :], a[:, 1, :],
                                                ALU.subtract).then_inc(s_sd, 1)
                def roots(q):
                    b4 = slice(q * QI, q * QI + QI)
                    pool.wait_ge(s_var2, g * 2 + q + 1)
                    nc.gpsimd.tensor_tensor(sm[:, 5, :, b4], sm[:, 2, :, b4], halves[0:HALF, :, b4], ALU.pow)
                    nc.gpsimd.tensor_tensor(sm[:, 6, :, b4], sm[:, 3, :, b4], halves[0:HALF, :, b4],
                                            ALU.pow).then_inc(s_root, 1)

                for b in range(GI):
                    pool.wait_ge(s_v, g * GI + b + 1)
                    if b >= 2:
                        pool.wait_ge(s_E, g * GI + b - 1)
                    u, a, c = u_spec[b % 2], v_own[b % 2], v_cross[b % 2]
                    nc.gpsimd.tensor_tensor(u[:, 0, :], a[:, 0, :], c[:, 1, :], ALU.add)
                    nc.gpsimd.tensor_tensor(u[:, 1, :], a[:, 1, :], c[:, 0, :], ALU.add).then_inc(s_u, 1)
                roots(0)
                roots(1)

            with pool.Fori(0, GROUPS - 1) as g:
                group(g)
            group(GROUPS - 1)

        @block.scalar
        def _(act):
            def x_evac(g, j):
                n = g * GRID + j
                for i in range(2):
                    if i == 0 and (j >= 2 or not isinstance(g, int) or g > 0):
                        act.wait_ge(s_tok, n - 1)
                    act.wait_ge(s_tr, 2 * n + i + 1)
                    nc.scalar.copy(x_t[j % 2][:, 3 * i:3 * i + 3, :],
                                   TR[i][:, 0:3 * GROWS].rearrange("p (q m) -> p q m", q=3)).then_inc(s_xt, 1)

            def patches(g, j):
                if j == 0:
                    act.wait_ge(s_x[0], 16 * g + 16)
                nc.scalar.copy(x_pat[j % 2][:, :].rearrange("p (r c) -> p r c", r=PATCH),
                               x_raw[0][:, :, j * PIX:(j + 1) * PIX]).then_inc(s_pat_a, 1)

            def spectra(g, b):
                act.wait_ge(s_A, g * GI + b + 1)
                nc.scalar.copy(spec[b][:, :, :],
                               P[b % 2][0:CH, 0:2 * TOK].rearrange("p (s k) -> p s k", s=2)).then_inc(s_spec, 1)

            def two_halves(bk, parts, n):
                return bk[0:parts, 0:2 * n].rearrange("p (c k) -> p c k", c=2)

            def head_step(g, q, step):
                pa, pb = (P[2], P[3]) if q == 0 else (P[0], P[1])
                act.wait_ge(s_zp, g * 10 + head_order("p", q, step) + 1)
                if step == 0:
                    nc.scalar.copy(zh[q][:, :], pa[:, 0:TOK]).then_inc(s_za, 1)
                elif step == 1:
                    nc.scalar.copy(zh_t[q][:, :, :], two_halves(pb, HALF, 128)).then_inc(s_za, 1)
                elif step == 2:
                    act.wait_ge(s_zv, g * 4 + head_order("v", q, 0) + 1)
                    nc.scalar.activation(z_e[q][:, :], pa[:, 0:TOK], ACT.Exp, bias=z_m[:, q, 0:1],
                                         accum_out=z_m[:, q, 1:2]).then_inc(s_za, 1)
                elif step == 3:
                    nc.scalar.copy(z_t[q][:, :, :], two_halves(pb, HALF, 128)).then_inc(s_za, 1)
                else:
                    c = pa[0:HALF, 0:3 * QI * HEADS].rearrange("p (k b h) -> p k b h", k=3, b=QI)
                    nc.scalar.copy(coef[q][:, 0:3, :, :], c)
                    nc.scalar.mul(coef[q][:, 3, :, :], c[:, 2], -1.0).then_inc(s_za, 1)

            def mixed(g, b):
                act.wait_ge(s_E, g * GI + b + 1)
                if b >= 2:
                    act.wait_ge(s_D, g * GI + b - 1)
                nc.scalar.copy(mix_t[b % 2][0:CH, :, :], two_halves(P[2], CH, TOK)).then_inc(s_mix, 1)

            def xn_evac(g, b):
                act.wait_ge(s_X, g * GI + b + 1)
                nc.scalar.copy(xn_t[b % 2][:, :, :], two_halves(P[b % 2], CH, TOK)).then_inc(s_xnt, 1)

            def logits(g, q):
                act.wait_ge(s_L, g * 2 + q + 1)
                nc.scalar.copy(lg[q][:, :], P[2 + q][:, 0:TOK]).then_inc(s_la, 1)
                act.wait_ge(s_lmax, g * 2 + q + 1)
                nc.scalar.activation(d_e[q][:, :], P[2 + q][:, 0:TOK], ACT.Exp, bias=d_m[:, q, 0:1],
                                     accum_out=d_m[:, q, 1:2]).then_inc(s_la, 1)

            def dispatch_evac(g, q):
                act.wait_ge(s_DT, g * 2 + q + 1)
                nc.scalar.copy(d_t[q][:, :, :], two_halves(P[1 + 2 * q], HALF, 128)).then_inc(s_dt, 1)

            def combine_exp(g, q):
                act.wait_ge(s_csub, g * 2 + q + 1)
                nc.scalar.activation(c_e[q][:, :, :], c_s[q][:, :, :], ACT.Exp).then_inc(s_cexp, 1)

            def combine_evac(g, q):
                act.wait_ge(s_CT, g * 2 + q + 1)
                nc.scalar.copy(c_t[q][:, :, :], two_halves(P[q], 128, HALF)).then_inc(s_ct, 1)

            def slots_evac(g, q):
                act.wait_ge(s_XST, g * 2 + q + 1)
                nc.scalar.copy(xs_t[:, :, q * QI:q * QI + QI].rearrange("p s b n m -> p s (b n m)"),
                               two_halves(P[2 + q], CH, 128)).then_inc(s_xst, 1)

            def gelu(g):
                act.wait_ge(s_DN, g + 1)
                for i in range(2):
                    last = nc.scalar.activation(hid[:, i, :], P[2][:, i * 32:i * 32 + 32], ACT.Gelu,
                                                bias=b_dn[:, i:i + 1])
                last.then_inc(s_gelu, 1)

            def y_evac(g, q):
                act.wait_ge(s_UP, g * 2 + q + 1)
                for b in range(QI):
                    at = slice(32 * b, 32 * b + 32)
                    last = nc.scalar.copy(y_blk[q][at, b, :], P[3 - q][at, 0:DIM])
                last.then_inc(s_yb, 1)

            def first_columns(g):
                patches(g, 0)
                patches(g, 1)
                for j in range(J_ACT):
                    x_evac(g, j)
                    if j + 2 < J_ACT:
                        patches(g, j + 2)

            def group(g, tok):
                def embed(j):
                    if tok:
                        x_evac(g + 1, j)
                if tok:
                    first_columns(g + 1)
                for b in range(4):
                    spectra(g, b)
                embed(4)
                head_step(g, 0, 0)
                spectra(g, 4)
                spectra(g, 5)
                head_step(g, 0, 1)
                spectra(g, 6)
                spectra(g, 7)
                head_step(g, 0, 2)
                embed(5)
                head_step(g, 1, 0)
                head_step(g, 0, 3)
                embed(6)
                head_step(g, 1, 1)
                head_step(g, 0, 4)
                head_step(g, 1, 2)
                embed(7)
                head_step(g, 1, 3)
                embed(8)
                head_step(g, 1, 4)
                embed(9)
                for b in range(GI):
                    mixed(g, b)
                embed(10)
                for b in range(GI):
                    xn_evac(g, b)
                    if b == 3:
                        logits(g, 0)
                        embed(11)
                logits(g, 1)
                dispatch_evac(g, 0)
                combine_exp(g, 0)
                embed(12)
                dispatch_evac(g, 1)
                combine_exp(g, 1)
                slots_evac(g, 0)
                embed(13)
                combine_evac(g, 0)
                slots_evac(g, 1)
                combine_evac(g, 1)
                gelu(g)
                y_evac(g, 0)
                y_evac(g, 1)

            first_columns(0)
            for j in range(J_ACT, GRID):
                x_evac(0, j)
            act.wait_ge(s_const, N_CONST)
            with act.Fori(0, GROUPS - 1) as g:
                group(g, True)
            group(GROUPS - 1, False)

        @block.vector
        def _(dve):
            links = [0]

            def patches(g, j):
                n = g * GRID + j
                s, w = j // 7, j % 7
                if j in (J_ACT, 7):
                    dve.wait_ge(s_x[s], 16 * g + 16)
                dve.wait_ge(s_tr, 2 * n - 2)
                nc.vector.tensor_copy(x_pat[j % 2][:, :].rearrange("p (r c) -> p r c", r=PATCH),
                                      x_raw[s][:, :, w * PIX:(w + 1) * PIX]).then_inc(s_pat_v, 1)

            def rows(g, j):
                dve.wait_ge(s_tok, g * GRID + j + 1)
                nc.vector.tensor_tensor(h_rows[:, j, :], HB[j % 2][0:GROWS, 0:DIM], b_tok[:, :],
                                        ALU.add).then_inc(s_rows, 1)

            def group(g, tok):
                links[0] = 0

                def link(ins):
                    links[0] += 1
                    ins.then_inc(s_vl, 1)
                    dve.wait_ge(s_vl, g * VECTOR_LINKS + links[0])

                def moments(b4, eps_at):
                    me, mo = st[:, :, b4, 1], st[:, :, b4, 4]
                    nc.vector.tensor_tensor(sm[:, 0, :, b4], me, mo, ALU.add)
                    nc.vector.tensor_tensor(sm[:, 4, :, b4], me, mo, ALU.subtract)
                    link(nc.vector.tensor_tensor(sm[:, 2, :, b4], st[:, :, b4, 2], st[:, :, b4, 5], ALU.add))
                    nc.vector.tensor_scalar(sm[:, 0, :, b4], sm[:, 0, :, b4], 0.5, None, ALU.mult)
                    nc.vector.tensor_scalar(sm[:, 2, :, b4], sm[:, 2, :, b4], 1.0 / DIM, None, ALU.mult)
                    link(nc.vector.scalar_tensor_tensor(sm[:, 4, :, b4], sm[:, 4, :, b4], 0.25,
                                                        sm[:, 4, :, b4], ALU.mult, ALU.mult))
                    link(nc.vector.tensor_tensor(sm[:, 2, :, b4], sm[:, 2, :, b4], sm[:, 4, :, b4], ALU.add))
                    return nc.vector.tensor_scalar(sm[:, 3, :, b4], sm[:, 2, :, b4], LN_EPS, None, ALU.add)

                def norm_stats(q):
                    for b in range(q * QI, q * QI + QI):
                        for c in range(2):
                            last = nc.vector.bn_stats(st[:, c, b, :], h[:, c, b, :])
                    link(last)
                    moments(slice(q * QI, q * QI + QI), 3).then_inc(s_var, 1)

                def norm(b):
                    if b >= 4:
                        dve.wait_ge(s_sd, g * GI + b - 3)
                    for c in range(2):
                        last = nc.vector.tensor_scalar(xln[b % 4][:, c, :], h[:, c, b, :], sm[:, 0, c, b:b + 1],
                                                       sm[:, 1, c, b:b + 1], ALU.subtract, ALU.mult)
                    last.then_inc(s_xln, 1)

                def head_max(q):
                    dve.wait_ge(s_zp, g * 10 + head_order("p", q, 2) + 1)
                    nc.vector.tensor_reduce(z_m[:, q, 0:1], (P[2], P[0])[q][:, 0:TOK], AX.X, ALU.max,
                                            negate=True).then_inc(s_zv, 1)

                def head_norm(q):
                    dve.wait_ge(s_za, g * 10 + head_order("a", q, 2) + 1)
                    link(nc.vector.reciprocal(z_m[:, q, 2:3], z_m[:, q, 1:2]))
                    nc.vector.tensor_scalar(z_n[q][:, :], z_e[q][:, :], z_m[:, q, 2:3], None,
                                            ALU.mult).then_inc(s_zv, 1)

                def products(b):
                    q, i = b // QI, b % QI
                    dve.wait_ge(s_B, g * GI + b + 1)
                    if b >= 2:
                        dve.wait_ge(s_u, g * GI + b - 1)
                    v = P[b % 2][0:HALF, 0:2 * DIM].rearrange("p (s h d) -> p s h d", s=2, d=HD)
                    for dst, c0 in ((v_own, 0), (v_cross, 2)):
                        co = coef_view(coef[q], c0, i)
                        last = nc.vector.tensor_tensor(dst[b % 2][:, :, :].rearrange("p s (h d) -> p s h d", d=HD),
                                                       v, co, ALU.mult)
                    last.then_inc(s_v, 1)

                def residual(b):
                    dve.wait_ge(s_D, g * GI + b + 1)
                    nc.vector.tensor_tensor(h1[:, :, b, :], P[3][0:HALF, 0:2 * DIM].rearrange("p (c d) -> p c d", c=2),
                                            h[:, :, b, :], ALU.add).then_inc(s_h1, 1)

                def stats2(b):
                    dve.wait_ge(s_h1, g * GI + b + 1)
                    for c in range(2):
                        last = nc.vector.bn_stats(st[:, c, b, :], h1[:, c, b, :])
                    return last

                def norm2_var(q):
                    b4 = slice(q * QI, q * QI + QI)
                    link(moments(b4, 3))
                    nc.vector.tensor_scalar(sm[:, 2, :, b4], sm[:, 2, :, b4], float(DIM), None,
                                            ALU.mult).then_inc(s_var2, 1)

                def norm2_scale(q):
                    b4 = slice(q * QI, q * QI + QI)
                    dve.wait_ge(s_root, g * 2 + q + 1)
                    link(nc.vector.scalar_tensor_tensor(sm[:, 7, :, b4], sm[:, 6, :, b4], L2_EPS,
                                                        sm[:, 5, :, b4], ALU.mult, ALU.add))
                    link(nc.vector.reciprocal(sm[:, 1, :, b4], sm[:, 7, :, b4]))

                def unit(b):
                    for c in range(2):
                        last = nc.vector.tensor_scalar(xn[:, b, c, :], h1[:, c, b, :], sm[:, 0, c, b:b + 1],
                                                       sm[:, 1, c, b:b + 1], ALU.subtract, ALU.mult)
                    last.then_inc(s_xn, 1)

                def slot_max(q):
                    dve.wait_ge(s_L, g * 2 + q + 1)
                    dve.wait_ge(s_la, g * 4 + 2 * q + 1)
                    nc.vector.tensor_reduce(d_m[:, q, 0:1], P[2 + q][:, 0:TOK], AX.X, ALU.max,
                                            negate=True).then_inc(s_lmax, 1)

                def slot_recip(q):
                    dve.wait_ge(s_la, g * 4 + 2 * q + 2)
                    link(nc.vector.reciprocal(d_m[:, q, 2:3], d_m[:, q, 1:2]))

                def combine_sub(q):
                    dve.wait_ge(s_LT, g * 2 + q + 1)
                    l_t = P[q][0:HALF, 0:256].rearrange("p (k s) -> p k s", s=SLOTS)
                    link(nc.vector.tensor_reduce(c_m[:, q, 0, :], l_t, AX.X, ALU.max))
                    nc.vector.tensor_tensor(c_s[q][:, :, :], l_t, spread(c_m[:, q, 0, :]),
                                            ALU.subtract).then_inc(s_csub, 1)

                def combine_norm(q):
                    dve.wait_ge(s_cexp, g * 2 + q + 1)
                    link(nc.vector.tensor_reduce(c_m[:, q, 1, :], c_e[q][:, :, :], AX.X, ALU.add))
                    link(nc.vector.reciprocal(c_m[:, q, 2, :], c_m[:, q, 1, :]))
                    nc.vector.tensor_tensor(c_n[q][:, :, :], c_e[q][:, :, :], spread(c_m[:, q, 2, :]),
                                            ALU.mult).then_inc(s_cn, 1)

                def slot_inputs(q):
                    dve.wait_ge(s_XS, g * 2 + q + 1)
                    nc.vector.tensor_scalar(xs[q][:, :], P[2 + q][:, 0:DIM], d_m[:, q, 2:3], None,
                                            ALU.mult).then_inc(s_xs, 1)

                def hidden_blocks():
                    dve.wait_ge(s_gelu, g + 1)
                    link(nc.vector.tensor_scalar(hid1[:, :, :], hid[:, :, :], one[:, 0:1], None, ALU.add))
                    for i in range(2):
                        last = nc.vector.tensor_tensor(hid_blk[:, i], over_experts(hid1[:, i, :]),
                                                       over_images(mask[:, i, :]), ALU.mult)
                    last.then_inc(s_blk, 1)

                def output(u):
                    q, c, pair = u // 4, (u // 2) % 2, u % 2
                    if u % 4 == 0:
                        dve.wait_ge(s_out, 16 + 64 * g)
                    dve.wait_ge(s_Y, g * 8 + u + 1)
                    b0 = q * QI + 2 * pair
                    nc.vector.tensor_tensor(o_sb[q][:, c, 2 * pair:2 * pair + 2, :],
                                            P[u % 2][0:HALF, 0:2 * DIM].rearrange("p (b d) -> p b d", b=2),
                                            h1[:, c, b0:b0 + 2, :], ALU.add).then_inc(s_o, 1)

                def fill(j):
                    if tok:
                        if J_ACT <= j < GRID:
                            patches(g + 1, j)
                        if j >= 2:
                            rows(g + 1, j - 2)

                dve.wait_ge(s_h[0], 128 * g + 128)
                norm_stats(0)
                dve.wait_ge(s_h[1], 128 * g + 128)
                fill(2)
                dve.wait_ge(s_rstd, g * 2 + 1)
                norm(0)
                norm(1)
                fill(3)
                norm(2)
                norm(3)
                norm_stats(1)
                fill(4)
                dve.wait_ge(s_rstd, g * 2 + 2)
                for b in range(4, 8):
                    norm(b)
                fill(5)
                head_max(0)
                fill(6)
                head_norm(0)
                fill(7)
                head_max(1)
                fill(8)
                head_norm(1)
                fill(9)
                products(0)
                products(1)
                fill(10)
                for b in range(2, GI):
                    products(b)
                    residual(b - 2)
                    last = stats2(b - 2)
                    if b == 5:
                        link(last)
                        norm2_var(0)
                residual(6)
                stats2(6)
                norm2_scale(0)
                unit(0)
                unit(1)
                residual(7)
                link(stats2(7))
                norm2_var(1)
                unit(2)
                unit(3)
                fill(11)
                slot_max(0)
                fill(12)
                norm2_scale(1)
                for b in range(4, 8):
                    unit(b)
                slot_recip(0)
                slot_max(1)
                combine_sub(0)
                slot_recip(1)
                fill(13)
                slot_inputs(0)
                combine_sub(1)
                combine_norm(0)
                fill(14)
                slot_inputs(1)
                combine_norm(1)
                hidden_blocks()
                if tok:
                    rows(g + 1, 13)
                for u in range(8):
                    output(u)
                assert links[0] == VECTOR_LINKS, links[0]

            dve.wait_ge(s_embed, 48)
            for j in range(GRID):
                if J_ACT <= j + 2 < GRID:
                    patches(0, j + 2)
                rows(0, j)
            dve.wait_ge(s_const, N_CONST)
            nc.vector.tensor_tensor(slots_sq[:, :, :], slots[:, :, :], slots[:, :, :], ALU.mult).then_inc(s_ready, 1)
            dve.wait_ge(s_ready, 1)
            nc.vector.tensor_reduce(slot_norm[:, 0], slots_sq[:, :, :].rearrange("p s (n m) -> p s m n", m=NP),
                                    AX.X, ALU.add).then_inc(s_ready, 1)
            dve.wait_ge(s_ready, 3)
            nc.vector.tensor_scalar(slot_norm[:, 2], slot_norm[:, 1], L2_EPS, None, ALU.add).then_inc(s_ready, 1)
            dve.wait_ge(s_ready, 4)
            nc.vector.reciprocal(slot_norm[:, 3], slot_norm[:, 2]).then_inc(s_ready, 1)
            dve.wait_ge(s_ready, 5)
            nc.vector.tensor_scalar(slot_norm[:, 0], slot_norm[:, 3], scale_c[:, 0:1], None,
                                    ALU.mult).then_inc(s_ready, 1)
            dve.wait_ge(s_ready, 6)
            for s in range(2):
                last = nc.vector.tensor_tensor(slots_n[:, s, :].rearrange("p (n m) -> p n m", m=NP),
                                               slots[:, s, :].rearrange("p (n m) -> p n m", m=NP),
                                               slot_norm[:, 0, s, :].unsqueeze(1).to_broadcast([CH, NE, NP]), ALU.mult)
            last.then_inc(s_ready, 1)

            with dve.Fori(0, GROUPS - 1) as g:
                group(g, True)
            group(GROUPS - 1, False)

        @block.tensor
        def _(pe):
            def mm(dst, lhsT, rhs, start=True, stop=True, **kw):
                return nc.tensor.matmul(dst, lhsT, rhs, start=start, stop=stop, **kw)

            def transpose_x(g, j):
                n = g * GRID + j
                if j < J_ACT:
                    pe.wait_ge(s_pat_a, g * J_ACT + j + 1)
                else:
                    pe.wait_ge(s_pat_v, g * J_VEC + j - J_ACT + 1)
                for i in range(2):
                    if j >= 1 or not isinstance(g, int) or g > 0:
                        pe.wait_ge(s_xt, 2 * n - 1 + i)
                    for q in range(3):
                        k = 3 * i + q
                        last = nc.tensor.transpose(TR[i][:, q * GROWS:(q + 1) * GROWS],
                                                   x_pat[j % 2][:, k * 128:(k + 1) * 128],
                                                   ident[0:GROWS, 0:GROWS])
                    last.then_inc(s_tr, 1)

            def embed_x(g, j):
                n = g * GRID + j
                if j >= 2 or not isinstance(g, int) or g > 0:
                    pe.wait_ge(s_rows, n - 1)
                for k in range(KQ):
                    if k % 3 == 0:
                        pe.wait_ge(s_xt, 2 * n + 1 + k // 3)
                    last = mm(HB[j % 2][0:GROWS, 0:DIM], x_t[j % 2][:, k, :], w_tok[:, k, :],
                              start=(k == 0), stop=(k == KQ - 1))
                last.then_inc(s_tok, 1)

            def group(g, tok):
                def tr(j):
                    if tok:
                        transpose_x(g + 1, j)

                def em(j):
                    if tok:
                        embed_x(g + 1, j)

                def forward(b):
                    pe.wait_ge(s_sd, g * GI + b + 1)
                    if b >= 2:
                        pe.wait_ge(s_spec, g * GI + b - 1)
                    dst = P[b % 2][0:CH, 0:2 * TOK].rearrange("p (s c k) -> p s c k", s=2, c=2)
                    for s in range(2):
                        for e in range(2):
                            last = mm(dst[:, s, :, e * QTR:(e + 1) * QTR], sumdif[b % 4][:, e, s * CH:(s + 1) * CH],
                                      fwd[:, e, :])
                    last.then_inc(s_A, 1)

                def head_step(q, step):
                    pa, pb = (P[2], P[3]) if q == 0 else (P[0], P[1])
                    if step == 0:
                        pe.wait_ge(s_spec, g * GI + 4 * q + 4)
                        for i in range(QI):
                            for s in range(2):
                                last = mm(pa[32 * i:32 * i + 32, 0:TOK], w_a[:, s, :], spec[4 * q + i][:, s, :],
                                          start=(s == 0), stop=(s == 1))
                    elif step == 1:
                        pe.wait_ge(s_za, g * 10 + head_order("a", q, 0) + 1)
                        for c in range(2):
                            last = nc.tensor.transpose(pb[0:HALF, c * 128:(c + 1) * 128],
                                                       zh[q][:, c * HALF:(c + 1) * HALF], ident[:, :])
                    elif step == 2:
                        pe.wait_ge(s_za, g * 10 + head_order("a", q, 1) + 1)
                        for c in range(2):
                            last = mm(pa[:, 0:TOK], zh_t[q][:, c, :], inv[:, c, :], start=(c == 0), stop=(c == 1))
                    elif step == 3:
                        pe.wait_ge(s_zv, g * 4 + head_order("v", q, 1) + 1)
                        for c in range(2):
                            last = nc.tensor.transpose(pb[0:HALF, c * 128:(c + 1) * 128],
                                                       z_n[q][:, c * HALF:(c + 1) * HALF], ident[:, :])
                    else:
                        pe.wait_ge(s_za, g * 10 + head_order("a", q, 3) + 1)
                        for k in range(3):
                            dst = pa[0:HALF, k * QI * HEADS:(k + 1) * QI * HEADS].rearrange("p (b h) -> p b h", b=QI)
                            for c in range(2):
                                rows_c = z_t[q][:, c, :].rearrange("p (b h) -> p b h", b=QI)[:, :, 0:HEADS]
                                last = mm(dst, headb[:, c, k, :], rows_c, start=(c == 0), stop=(c == 1))
                    last.then_inc(s_zp, 1)

                def values(b):
                    if b < 2:
                        pe.wait_ge(s_za, g * 10 + 10)
                    else:
                        pe.wait_ge(s_v, g * GI + b - 1)
                    for c in range(2):
                        for s in range(2):
                            last = mm(P[b % 2][0:HALF, c * DIM:(c + 1) * DIM], spec[b][:, s, c * HALF:(c + 1) * HALF],
                                      w_v[:, s, :], start=(s == 0), stop=(s == 1))
                    last.then_inc(s_B, 1)

                def inverse(b):
                    pe.wait_ge(s_u, g * GI + b + 1)
                    if b >= 1:
                        pe.wait_ge(s_mix, g * GI + b)
                    for s in range(2):
                        for c in range(2):
                            last = mm(P[2][0:CH, s * TOK:(s + 1) * TOK], u_spec[b % 2][:, c, s * CH:(s + 1) * CH],
                                      inv[:, c, :], start=(c == 0), stop=(c == 1))
                    last.then_inc(s_E, 1)

                def project(b):
                    pe.wait_ge(s_mix, g * GI + b + 1)
                    if b >= 1:
                        pe.wait_ge(s_h1, g * GI + b)
                    for c in range(2):
                        tk = slice(c * HALF, (c + 1) * HALF)
                        mm(P[3][0:HALF, c * DIM:(c + 1) * DIM], mix_t[b % 2][0:CH, 0, tk], w_p[0:CH, 0, :], stop=False)
                        last = mm(P[3][0:HALF, c * DIM:(c + 1) * DIM], mix_t[b % 2][:, 1, tk], w_p[:, 1, :],
                                  start=False)
                    last.then_inc(s_D, 1)

                def turn_units(b):
                    pe.wait_ge(s_xn, g * GI + b + 1)
                    if b >= 2:
                        pe.wait_ge(s_xnt, g * GI + b - 1)
                    for s in range(2):
                        for c in range(2):
                            at = s * TOK + c * HALF
                            last = nc.tensor.transpose(P[b % 2][0:CH, at:at + HALF], xn[:, b, c, s * CH:(s + 1) * CH],
                                                       ident[0:HALF, 0:HALF])
                    last.then_inc(s_X, 1)

                def logits(b):
                    q, i = b // QI, b % QI
                    pe.wait_ge(s_xnt, g * GI + b + 1)
                    for s in range(2):
                        last = mm(P[2 + q][32 * i:32 * i + 32, 0:TOK], slots_n[:, s, :], xn_t[b % 2][:, s, :],
                                  start=(s == 0), stop=(s == 1))
                    if i == QI - 1:
                        last.then_inc(s_L, 1)

                def turn_logits(q):
                    pe.wait_ge(s_la, g * 4 + 2 * q + 1)
                    for c in range(2):
                        last = nc.tensor.transpose(P[q][0:HALF, c * 128:(c + 1) * 128],
                                                   lg[q][:, c * HALF:(c + 1) * HALF], ident[:, :])
                    last.then_inc(s_LT, 1)

                def turn_dispatch(q):
                    pe.wait_ge(s_la, g * 4 + 2 * q + 2)
                    for c in range(2):
                        last = nc.tensor.transpose(P[1 + 2 * q][0:HALF, c * 128:(c + 1) * 128],
                                                   d_e[q][:, c * HALF:(c + 1) * HALF], ident[:, :])
                    last.then_inc(s_DT, 1)

                def slot_inputs(q):
                    pe.wait_ge(s_dt, g * 2 + q + 1)
                    for i in range(QI):
                        for c in range(2):
                            last = mm(P[2 + q][32 * i:32 * i + 32, 0:DIM], d_t[q][:, c, 32 * i:32 * i + 32],
                                      xn[:, 4 * q + i, c, :], start=(c == 0), stop=(c == 1))
                    last.then_inc(s_XS, 1)

                def turn_slots(q):
                    pe.wait_ge(s_xs, g * 2 + q + 1)
                    for s in range(2):
                        last = nc.tensor.transpose(P[2 + q][0:CH, s * 128:(s + 1) * 128],
                                                   xs[q][:, s * CH:(s + 1) * CH], ident[:, :])
                    last.then_inc(s_XST, 1)

                def turn_combine(q):
                    pe.wait_ge(s_cn, g * 2 + q + 1)
                    for c in range(2):
                        last = nc.tensor.transpose(P[q][:, c * HALF:(c + 1) * HALF],
                                                   c_n[q][:, c * QI:(c + 1) * QI, :].rearrange("p b s -> p (b s)"),
                                                   ident[0:HALF, 0:HALF])
                    last.then_inc(s_CT, 1)

                def expert_down():
                    pe.wait_ge(s_xst, g * 2 + 2)
                    for n in range(NE):
                        i = n // 4
                        for s in range(2):
                            last = mm(P[2][32 * (n % 4):32 * (n % 4) + 32, 32 * i:32 * i + 32].rearrange(
                                "p (b m) -> p b m", m=NP), w_dn[:, s, n, :], xs_t[:, s, :, n, :],
                                start=(s == 0), stop=(s == 1))
                    last.then_inc(s_DN, 1)

                def expert_up(q):
                    if q == 0:
                        pe.wait_ge(s_blk, g + 1)
                    for i in range(2):
                        last = mm(P[3 - q][:, 0:DIM], hid_blk[:, i, 4 * q:4 * q + 4].rearrange("p b n m -> p (b n m)"),
                                  w_up[:, i, :], start=(i == 0), stop=(i == 1))
                    last.then_inc(s_UP, 1)

                def combine(u):
                    q, c, pair = u // 4, (u // 2) % 2, u % 2
                    if u == 0:
                        pe.wait_ge(s_ct, g * 2 + 2)
                        pe.wait_ge(s_yb, g * 2 + 1)
                    if u == 4:
                        pe.wait_ge(s_yb, g * 2 + 2)
                    if u >= 2:
                        pe.wait_ge(s_o, g * 8 + u - 1)
                    mm(P[u % 2][0:HALF, 0:2 * DIM], c_t[q][:, c, :],
                       y_blk[q][:, 2 * pair:2 * pair + 2, :].rearrange("p b d -> p (b d)")).then_inc(s_Y, 1)

                def fill(j):
                    tr(j)
                    if j >= 1:
                        em(j - 1)

                for j in range(4):
                    fill(j)
                for b in range(4):
                    forward(b)
                fill(4)
                head_step(0, 0)
                forward(4)
                forward(5)
                head_step(0, 1)
                forward(6)
                forward(7)
                head_step(0, 2)
                fill(5)
                head_step(1, 0)
                head_step(0, 3)
                fill(6)
                head_step(1, 1)
                head_step(0, 4)
                head_step(1, 2)
                fill(7)
                head_step(1, 3)
                fill(8)
                head_step(1, 4)
                values(0)
                values(1)
                fill(9)
                for b in range(GI):
                    inverse(b)
                    if b + 2 < GI:
                        values(b + 2)
                    if b >= 1:
                        project(b - 1)
                    if b == 6:
                        tr(10)
                em(9)
                project(7)
                for q in range(2):
                    turn_units(4 * q)
                    for b in range(4 * q + 1, 4 * q + 4):
                        turn_units(b)
                        logits(b - 1)
                    logits(4 * q + 3)
                    if q == 0:
                        fill(11)
                        tr(12)
                turn_logits(0)
                turn_dispatch(0)
                em(11)
                slot_inputs(0)
                turn_logits(1)
                turn_dispatch(1)
                turn_slots(0)
                fill(13)
                slot_inputs(1)
                turn_combine(0)
                turn_slots(1)
                turn_combine(1)
                expert_down()
                em(13)
                expert_up(0)
                expert_up(1)
                for u in range(8):
                    combine(u)

            pe.wait_ge(s_embed, 48)
            transpose_x(0, 0)
            for j in range(GRID):
                if j + 1 < GRID:
                    transpose_x(0, j + 1)
                embed_x(0, j)
            pe.wait_ge(s_const, N_CONST)
            pe.wait_ge(s_zero, 1)
            pe.wait_ge(s_ready, 7)
            with pe.Fori(0, GROUPS - 1) as g:
                group(g, True)
            group(GROUPS - 1, False)


HEAD_STEPS = [(0, 0), (0, 1), (0, 2), (1, 0), (0, 3), (1, 1), (0, 4), (1, 2), (1, 3), (1, 4)]
HEAD_VECTOR = [(0, 0), (0, 1), (1, 0), (1, 1)]


def head_order(engine, q, step):
    return (HEAD_VECTOR if engine == "v" else HEAD_STEPS).index((q, step))


def coef_view(c, first, image):
    v = c[:, first:first + 2, image, :]
    return v.unsqueeze(3).to_broadcast([HALF, 2, HEADS, HD])


def spread(v):
    return v.unsqueeze(2).to_broadcast([HALF, 2 * QI, SLOTS])


def over_experts(v):
    return v.rearrange("p (b o m) -> p b o m", o=1, m=NP).to_broadcast([128, GI, NE, NP])


def over_images(v):
    return v.rearrange("p (o n m) -> p o n m", o=1, m=NP).to_broadcast([128, GI, NE, NP])


_INS = ["x", "L0_tok_W", "L0_tok_b", "L0_attn_W_A", "L0_attn_W_V", "L0_attn_W_proj", "L0_attn_b_proj",
        "L0_ffn_slot_params", "L0_ffn_scale", "L0_ffn_W_down", "L0_ffn_b_down", "L0_ffn_W_up", "L0_ffn_b_up"]


def kernel(**inputs):
    import concourse.bacc as bacc
    from concourse.bass_utils import run_bass_kernel_spmd

    nc = bacc.Bacc("TRN2", target_bir_lowering=False, num_devices=1)
    arrays, args = {}, []
    for name in _INS:
        a = np.ascontiguousarray(inputs[name])
        if a.ndim == 0 or name == "L0_ffn_scale":
            a = a.reshape(1, 1)
        arrays[f"in_{name}"] = a
    for name, a in tables().items():
        arrays[f"table_{name}"] = a
    for name, a in arrays.items():
        args.append(nc.dram_tensor(name, a.shape, mybir.dt.from_np(a.dtype), kind="ExternalInput").ap())
    args.append(nc.dram_tensor("out", (IMAGES, TOK, DIM), F32, kind="ExternalOutput").ap())
    build(nc, *args)
    r = run_bass_kernel_spmd(nc, [arrays], core_ids=[0])
    return r.results[0]["out"]
```

```python
import numpy as np
from contextlib import ExitStack

import concourse.bass as bass
from concourse import mybir
from concourse.alu_op_type import AluOpType as ALU

F32 = mybir.dt.float32
F32R = mybir.dt.float32r
ACT = mybir.ActivationFunctionType
AX = mybir.AxisListType

IMAGES, SIDE, PATCH, COLORS = 64, 224, 16, 3
GRID = SIDE // PATCH
TOK = GRID * GRID
HALF = TOK // 2
QTR = HALF // 2
DIM = 192
CH = DIM // 2
PIX = PATCH * COLORS
PDIM = PATCH * PIX
KQ = PDIM // 128
HEADS = 12
HD = DIM // HEADS
GI = 8
GROUPS = IMAGES // GI
GROWS = GI * GRID
QI = 4
NE, NP = 8, 4
SLOTS = NE * NP
HID = DIM // 8
J_ACT = 4
J_VEC = GRID - J_ACT
LN_EPS, L2_EPS = 1e-5, 1e-6


def tables():
    j = np.arange(HALF)[:, None]
    k_even, k_odd = 2 * np.arange(QTR), 2 * np.arange(QTR) + 1

    def cos_sin(tokens, cos_k, sin_k):
        w = 2 * np.pi / TOK
        return np.cos(w * tokens * cos_k), np.sin(w * tokens * sin_k)

    k = np.concatenate([k_even, k_odd])
    even_c, even_s = cos_sin(j, k_even[None], k_even[None])
    even_s[:, 0] = (-1.0) ** j[:, 0]
    odd_c, odd_s = cos_sin(j, k_odd[None], k_odd[None])
    forward = np.stack([np.concatenate([even_c, even_s], 1), np.concatenate([odd_c, odd_s], 1)], 1)
    t = np.arange(TOK)
    inv_c, inv_s = cos_sin(t[None], k[:, None], k[:, None])
    weight = np.where(k == 0, 1.0, 2.0)[:, None] / TOK
    inv_c, inv_s = inv_c * weight, inv_s * weight
    inv_s[0] = (-1.0) ** t / TOK
    inverse = np.stack([inv_c, inv_s], 1)
    all_c, all_s = cos_sin(t[:, None], k[None], k[None])
    own_s = all_c.copy()
    own_s[:, 0] = (-1.0) ** t
    heads = np.stack([all_c, own_s, -all_s], 1) / TOK
    heads = heads.reshape(2, HALF, 3, HALF).transpose(1, 0, 2, 3)
    mask = np.zeros((128, 2, NE, NP))
    one = np.zeros((128, 1))
    for n in range(NE):
        mask[32 * (n % 4):32 * (n % 4) + HID + 1, n // 4, n, :] = 1.0
        one[32 * (n % 4) + HID] = 1.0
    out = {"ident": np.eye(128), "forward": forward, "inverse": inverse, "heads": heads,
           "mask": mask.reshape(128, 2, SLOTS), "one": one}
    return {n: np.ascontiguousarray(a, dtype=np.float32) for n, a in out.items()}


def build(nc, x, tok_W, tok_b, W_A, W_V, W_proj, b_proj, slot_params, scale, W_down, b_down, W_up,
          b_up, t_ident, t_forward, t_inverse, t_heads, t_mask, t_one, out):
    ctx = ExitStack()
    with ctx:
        def sb(name, shape, dtype=F32):
            return ctx.enter_context(nc.sbuf_tensor(name, shape, dtype))

        def sb_parts(name, shape):
            return [sb(name + part, shape, F32R) for part in ("_hi", "_lo")]

        def sem(name):
            return ctx.enter_context(nc.semaphore(name))

        ident = sb("ident", [128, 128])
        fwd = sb("fwd", [HALF, 2, HALF])
        inv = sb("inv", [HALF, 2, TOK])
        headb = sb("headb", [HALF, 2, 3, HALF])
        mask = sb("mask", [128, 2, SLOTS])
        one = sb("one", [128, 1])
        w_tok = sb("w_tok", [128, KQ, DIM])
        b_tok = sb("b_tok", [GROWS, DIM])
        w_a = sb("w_a", [CH, 2, 32])
        w_v = sb("w_v", [CH, 2, DIM])
        w_p = sb("w_p", [CH + 1, 2, DIM])
        w_v_parts = sb_parts("w_v", [CH, 2, DIM])
        w_p_parts = sb_parts("w_p", [CH + 1, 2, DIM])
        inv_parts = sb_parts("inv", [HALF, 2, TOK])
        slots = sb("slots", [CH, 2, SLOTS])
        slots_sq = sb("slots_sq", [CH, 2, SLOTS])
        slot_norm = sb("slot_norm", [CH, 4, 2, NP])
        slots_n = sb("slots_n", [CH, 2, SLOTS])
        scale_c = sb("scale_c", [CH, 1])
        halves = sb("halves", [128, 2, 2, QI])
        neg_halves = sb("neg_halves", [128, 2, QI])
        w_dn = sb("w_dn", [CH, 2, NE, 32])
        w_up = sb("w_up", [128, 2, DIM])
        b_dn = sb("b_dn", [128, 2])

        x_raw = [sb(f"x_raw{i}", [GROWS, PATCH, GRID // 2 * PIX]) for i in range(2)]
        x_pat = [sb(f"x_pat{i}", [GROWS, PDIM]) for i in range(2)]
        x_t = [sb(f"x_t{i}", [128, KQ, GROWS]) for i in range(2)]
        h_rows = sb("h_rows", [GROWS, GRID, DIM])
        h = sb("h", [HALF, 2, GI, DIM])
        h1_rows = sb("h1_rows", [GROWS, 2 * GI * DIM])
        h1 = h1_rows[0:HALF, :].rearrange("p (c b d) -> p c b d", c=2, b=GI)
        first_rows = h1_rows[:, 0:GRID * DIM].rearrange("p (j d) -> p j d", d=DIM)
        st = sb("st", [HALF, 2, QI, 6])
        sm = sb("sm", [HALF, 5, 2, QI])
        xln = [sb(f"xln{i}", [HALF, 2, DIM]) for i in range(QI)]
        sumdif = [sb(f"sumdif{i}", [HALF, 2, DIM]) for i in range(QI)]
        spec = [sb(f"spec{i}", [CH, 2, TOK]) for i in range(QI)]
        spec_parts = [sb_parts(f"spec{i}", [CH, 2, TOK]) for i in range(QI)]
        zh = sb("zh", [128, TOK])
        zh_t = sb("zh_t", [HALF, 2, 128])
        z_e = sb("z_e", [128, TOK])
        z_n = sb("z_n", [128, TOK])
        z_m = sb("z_m", [128, 3])
        z_t = sb("z_t", [HALF, 2, 128])
        coef = sb("coef", [HALF, 4, QI, HEADS])
        v_own = [sb(f"v_own{i}", [HALF, 2, DIM]) for i in range(2)]
        v_cross = [sb(f"v_cross{i}", [HALF, 2, DIM]) for i in range(2)]
        u_spec = [sb(f"u_spec{i}", [HALF, 2, DIM]) for i in range(2)]
        u_parts = [sb_parts(f"u_spec{i}", [HALF, 2, DIM]) for i in range(2)]
        mix_parts = [sb_parts(f"mix_t{i}", [CH + 1, 2, TOK]) for i in range(2)]
        st2 = sb("st2", [HALF, 2, QI, 6])
        sm2 = sb("sm2", [HALF, 8, 2, QI])
        xn = sb("xn", [HALF, QI, 2, DIM])
        xn_t = [sb(f"xn_t{i}", [CH, 2, TOK]) for i in range(2)]
        lg = sb("lg", [128, TOK])
        d_e = sb("d_e", [128, TOK])
        d_m = sb("d_m", [128, 3])
        d_t = sb("d_t", [HALF, 2, 128])
        c_s = sb("c_s", [HALF, 2 * QI, SLOTS])
        c_e = sb("c_e", [HALF, 2 * QI, SLOTS])
        c_n = sb("c_n", [HALF, 2 * QI, SLOTS])
        c_m = sb("c_m", [HALF, 3, 2 * QI])
        c_t = sb("c_t", [128, 2, HALF])
        xs = sb("xs", [128, DIM])
        xs_t = sb("xs_t", [CH, 2, QI, NE, NP])
        hid = sb("hid", [128, 2, QI * NP])
        hid1 = sb("hid1", [128, 2, QI * NP])
        hid_blk = sb("hid_blk", [128, 2, QI, NE, NP])
        y_blk = sb("y_blk", [128, QI, DIM])
        o_sb = [sb(f"o_sb{i}", [HALF, 2, QI, DIM]) for i in range(2)]

        bank = [ctx.enter_context(nc.psum_tensor(f"bank{i}", [128, 512], F32)) for i in range(8)]
        TR, HB, P, F = bank[0], bank[1], bank[2:6], bank[6:8]

        s_embed = sem("s_embed")
        s_const = sem("s_const")
        s_zero = sem("s_zero")
        s_pool = sem("s_pool")
        s_ready = sem("s_ready")
        s_x = [sem(f"s_x{i}") for i in range(2)]
        s_x_first = sem("s_x_first")
        s_pat_a = sem("s_pat_a")
        s_pat_v = sem("s_pat_v")
        s_tr = sem("s_tr")
        s_xt = sem("s_xt")
        s_tok = sem("s_tok")
        s_rows = sem("s_rows")
        s_h = [sem(f"s_hq{i}") for i in range(2)]
        s_var = sem("s_var")
        s_rstd = sem("s_rstd")
        s_xln = sem("s_xln")
        s_sd = sem("s_sd")
        s_A = sem("s_A")
        s_spec = sem("s_spec")
        s_spec_lo = sem("s_spec_lo")
        s_parts = sem("s_parts")
        s_u_hi = sem("s_u_hi")
        s_u_lo = sem("s_u_lo")
        s_mix_lo = sem("s_mix_lo")
        s_zp = sem("s_zp")
        s_za = sem("s_za")
        s_zv = sem("s_zv")
        s_B = sem("s_B")
        s_v = sem("s_v")
        s_u = sem("s_u")
        s_E = sem("s_E")
        s_mix = sem("s_mix")
        s_D = sem("s_D")
        s_h1 = sem("s_h1")
        s_var2 = sem("s_var2")
        s_root = sem("s_root")
        s_xn = sem("s_xn")
        s_X = sem("s_X")
        s_xnt = sem("s_xnt")
        s_L = sem("s_L")
        s_lmax = sem("s_lmax")
        s_la = sem("s_la")
        s_LT = sem("s_LT")
        s_DT = sem("s_DT")
        s_dt = sem("s_dt")
        s_csub = sem("s_csub")
        s_cexp = sem("s_cexp")
        s_cn = sem("s_cn")
        s_CT = sem("s_CT")
        s_ct = sem("s_ct")
        s_XS = sem("s_XS")
        s_xs = sem("s_xs")
        s_XST = sem("s_XST")
        s_xst = sem("s_xst")
        s_DN = sem("s_DN")
        s_gelu = sem("s_gelu")
        s_blk = sem("s_blk")
        s_UP = sem("s_UP")
        s_yb = sem("s_yb")
        s_Y = sem("s_Y")
        s_o = sem("s_o")
        s_out = [sem(f"s_out{i}") for i in range(2)]
        s_vn = sem("s_vn")
        s_vh = sem("s_vh")
        s_vf = sem("s_vf")

        x_v = x.rearrange("b (i r) (s w) c -> s (b i) r (w c)", r=PATCH, s=2)
        out_v = out.rearrange("(q b) (c p) d -> q p c b d", b=QI, p=HALF)

        first = [
            (ident[:, :], t_ident), (w_tok[:, :, :], tok_W.rearrange("(q p) e -> p q e", p=128)),
            (b_tok[:, :], tok_b.rearrange("(o e) -> o e", o=1).to_broadcast([GROWS, DIM])),
        ]
        consts = [
            (fwd[:, :, :], t_forward), (inv[:, :, :], t_inverse),
            (headb[:, :, :, :], t_heads), (mask[:, :, :], t_mask), (one[:, :], t_one),
            (w_v[:, :, :], W_V.rearrange("(s p) e -> p s e", p=CH)),
            (w_p[0:CH, :, :], W_proj.rearrange("(s p) e -> p s e", p=CH)),
            (w_p[CH:CH + 1, 1, :], b_proj.rearrange("(o e) -> o e", o=1)),
            (slots[:, :, :], slot_params.rearrange("(s p) n m -> p s (n m)", p=CH)),
            (scale_c[:, :], scale.to_broadcast([CH, 1])),
        ]
        padded = [(w_a[:, :, 0:HEADS], W_A.rearrange("(s p) e -> p s e", p=CH))]
        for s in range(2):
            padded.append((w_dn[:, s, :, 0:HID], W_down[:, s * CH:(s + 1) * CH, :].rearrange("n p m -> p n m")))
        for n in range(NE):
            at = 32 * (n % 4)
            padded.append((w_up[at:at + HID, n // 4, :], W_up[n]))
            padded.append((w_up[at + HID:at + HID + 1, n // 4, :], b_up[n:n + 1, :]))
            padded.append((b_dn[at:at + HID, n // 4:n // 4 + 1], b_down[n:n + 1, :].rearrange("o m -> m o")))
        N_CONST = 16 * (len(consts) + len(padded))

        block = ctx.enter_context(nc.Block())

        @block.sync
        def _(sp):
            def held(*values):
                return [v if isinstance(v, int) else sp.snap(v) for v in values]

            def group(g, load, move, before=True):
                x_row, x_out0, x_out1, out_a, out_b = held(
                    (g + 2) * GROWS, (g + 1) * J_VEC + GRID // 2 - J_ACT, (g + 1) * J_VEC + J_VEC, 2 * g - 1, 2 * g)
                rows_in, h_out1, o_a, o_b = held((g + 2) * GRID, g * GI + GI, 8 * g, 8 * g + 4)

                def load_x(s):
                    sp.wait_ge(s_pat_v, (x_out0, x_out1)[s])
                    sp.dma_start(x_raw[s][:, :, :], x_v[s, bass.ds(x_row, GROWS)]).then_inc(s_x[s], 16)

                def store(quad, outputs, q):
                    sp.wait_ge(s_o, outputs)
                    for c in range(2):
                        sp.dma_start(out_v[bass.ds(quad, 1), :, c].rearrange("o p b d -> (o p) b d"),
                                     o_sb[q][:, c, :, :]).then_inc(s_out[q], 16)

                if load:
                    load_x(0)
                if before:
                    store(out_a, o_a, 1)
                if load:
                    load_x(1)
                if move:
                    sp.wait_ge(s_rows, rows_in)
                    move_h(0)
                store(out_b, o_b, 0)
                if move:
                    sp.wait_ge(s_h1, h_out1)
                    move_h(1)

            def move_h(q, src=h_rows):
                for b in range(q * QI, q * QI + QI):
                    for c in range(2):
                        r0 = b * GRID + c * (GRID // 2)
                        sp.dma_start(h[:, c, b, :], src[r0:r0 + GRID // 2, :, :]).then_inc(s_h[q], 16)

            for dst, src in first[:1]:
                sp.dma_start(dst, src).then_inc(s_embed, 16)
            sp.dma_start(x_raw[0][:, :, 0:2 * PIX], x_v[0, 0:GROWS, :, 0:2 * PIX]).then_inc(s_x_first, 16)
            for dst, src in first[1:]:
                sp.dma_start(dst, src).then_inc(s_embed, 16)
            sp.dma_start(x_raw[0][:, :, 2 * PIX:], x_v[0, 0:GROWS, :, 2 * PIX:]).then_inc(s_x[0], 16)
            sp.dma_start(x_raw[1][:, :, :], x_v[1, 0:GROWS]).then_inc(s_x[1], 16)
            for dst, src in consts:
                sp.dma_start(dst, src).then_inc(s_const, 16)
            sp.wait_ge(s_zero, 1)
            for dst, src in padded:
                sp.dma_start(dst, src).then_inc(s_const, 16)
            for q in range(2):
                sp.sem_inc(s_out[q], 16)
            for half in range(2):
                sp.wait_ge(s_pat_v, (GRID // 2 - J_ACT, J_VEC)[half])
                sp.dma_start(x_raw[half][:, :, :], x_v[half, GROWS:2 * GROWS]).then_inc(s_x[half], 16)
            sp.wait_ge(s_rows, GRID)
            move_h(0, first_rows)
            move_h(1, first_rows)
            group(0, True, True, before=False)
            with sp.Fori(1, GROUPS - 2) as g:
                group(g, True, True)
            group(GROUPS - 2, False, True)
            group(GROUPS - 1, False, False)
            sp.wait_ge(s_o, GROUPS * 8)
            for c in range(2):
                sp.dma_start(out_v[2 * GROUPS - 1, :, c], o_sb[1][:, c, :, :]).then_inc(s_out[1], 16)
            for q in range(2):
                sp.wait_ge(s_out[q], 16 + GROUPS * 32)

        @block.gpsimd
        def _(pool):
            for t in (w_a, w_dn, w_up, b_dn, y_blk):
                nc.gpsimd.memset(t[...], 0.0)
            nc.gpsimd.memset(halves[:, :, :, :], 0.5)
            nc.gpsimd.memset(neg_halves[:, :, :], -0.5).then_inc(s_pool, 1)
            pool.wait_ge(s_pool, 1)
            nc.gpsimd.memset(w_p[CH:CH + 1, 0, :], 0.0)
            nc.gpsimd.memset(mix_parts[0][0][CH:CH + 1, :, :].bitcast(F32), 1.0)
            nc.gpsimd.memset(mix_parts[1][0][CH:CH + 1, :, :].bitcast(F32), 1.0).then_inc(s_zero, 1)
            def halves_sums(g, q):
                quad = 2 * g + q
                pool.wait_ge(s_var, quad + 1)
                nc.gpsimd.tensor_tensor(sm[:, 1, :, :], sm[:, 3, :, :], neg_halves[0:HALF, :, :],
                                        ALU.pow).then_inc(s_rstd, 1)
                for i in range(QI):
                    pool.wait_ge(s_xln, quad * QI + i + 1)
                    if not isinstance(quad, int) or quad > 0:
                        pool.wait_ge(s_A, quad * QI + i - 3)
                    a = xln[i]
                    nc.gpsimd.tensor_tensor(sumdif[i][:, 0, :], a[:, 0, :], a[:, 1, :], ALU.add)
                    nc.gpsimd.tensor_tensor(sumdif[i][:, 1, :], a[:, 0, :], a[:, 1, :],
                                            ALU.subtract).then_inc(s_sd, 1)

            def roots(quad):
                pool.wait_ge(s_var2, quad + 1)
                nc.gpsimd.tensor_tensor(sm2[:, 5:7, :, :], sm2[:, 2:4, :, :], halves[0:HALF, :, :, :],
                                        ALU.pow).then_inc(s_root, 1)

            def spectra_low(quad):
                for i in range(QI):
                    b = quad * QI + i
                    pool.wait_ge(s_spec, b + 1)
                    if not isinstance(quad, int) or quad > 0:
                        pool.wait_ge(s_B, b - 3)
                    hi, lo = spec_parts[i]
                    nc.gpsimd.tensor_tensor(lo[:, :, :], spec[i][:, :, :], hi[:, :, :].bitcast(F32),
                                            ALU.subtract).then_inc(s_spec_lo, 1)

            def spectra_sums(quad):
                for i in range(QI):
                    b = quad * QI + i
                    pool.wait_ge(s_v, b + 1)
                    if i >= 2 or not isinstance(quad, int) or quad > 0:
                        pool.wait_ge(s_u_lo, b - 1)
                    nc.gpsimd.tensor_tensor(u_spec[i % 2][:, :, :], v_own[i % 2][:, :, :], v_cross[i % 2][:, :, :],
                                            ALU.add).then_inc(s_u, 1)

            def group(g, before, after):
                if before:
                    roots(2 * g - 1)
                spectra_low(2 * g)
                halves_sums(g, 1)
                spectra_sums(2 * g)
                roots(2 * g)
                spectra_low(2 * g + 1)
                spectra_sums(2 * g + 1)
                if after:
                    halves_sums(g + 1, 0)

            halves_sums(0, 0)
            pool.wait_ge(s_zero, 1)
            pool.wait_ge(s_ready, 2)
            nc.gpsimd.tensor_tensor(slot_norm[:, 1], slot_norm[:, 0], halves[0:CH, 0, :, :], ALU.pow).then_inc(s_ready, 1)
            group(0, False, True)
            with pool.Fori(1, GROUPS - 1) as g:
                group(g, True, True)
            group(GROUPS - 1, True, False)
            roots(2 * GROUPS - 1)

        @block.scalar
        def _(act):
            def x_evac(g, j, halves=(0, 1), start=False):
                n = g * GRID + j
                for i in halves:
                    if i == 0 and (j >= 2 or not isinstance(g, int) or g > 0):
                        act.wait_ge(s_tok, n - 1)
                    act.wait_ge(s_tr, 2 * n + i + 1)
                    src = (TR, F[0])[i] if start else TR
                    nc.scalar.copy(x_t[j % 2][:, 3 * i:3 * i + 3, :],
                                   src[:, 0:3 * GROWS].rearrange("p (q m) -> p q m", q=3)).then_inc(s_xt, 1)

            def patches(g, j):
                if isinstance(g, int) and g == 0:
                    act.wait_ge((s_x_first, s_x[0])[j // 2], 16)
                elif j == 0:
                    act.wait_ge(s_x[0], 16 * g + 16)
                nc.scalar.copy(x_pat[j % 2][:, :].rearrange("p (r c) -> p r c", r=PATCH),
                               x_raw[0][:, :, j * PIX:(j + 1) * PIX]).then_inc(s_pat_a, 1)

            def two_halves(bk, parts, n):
                return bk[0:parts, 0:2 * n].rearrange("p (c k) -> p c k", c=2)

            def spectra(quad, i):
                act.wait_ge(s_A, quad * QI + i + 1)
                src = P[i % 2][0:CH, 0:2 * TOK].rearrange("p (s k) -> p s k", s=2)
                nc.scalar.copy(spec[i][:, :, :], src)
                nc.scalar.copy(spec_parts[i][0][:, :, :], src).then_inc(s_spec, 1)

            def head_step(quad, step):
                act.wait_ge(s_zp, quad * 5 + step + 1)
                if step == 0:
                    nc.scalar.copy(zh[:, :], P[0][:, 0:TOK]).then_inc(s_za, 1)
                elif step == 1:
                    nc.scalar.copy(zh_t[:, :, :], two_halves(P[1], HALF, 128)).then_inc(s_za, 1)
                elif step == 2:
                    act.wait_ge(s_zv, quad * 2 + 1)
                    nc.scalar.activation(z_e[:, :], P[0][:, 0:TOK], ACT.Exp, bias=z_m[:, 0:1],
                                         accum_out=z_m[:, 1:2]).then_inc(s_za, 1)
                elif step == 3:
                    nc.scalar.copy(z_t[:, :, :], two_halves(P[1], HALF, 128)).then_inc(s_za, 1)
                else:
                    c = P[0][0:HALF, 0:3 * QI * HEADS].rearrange("p (k b h) -> p k b h", k=3, b=QI)
                    nc.scalar.copy(coef[:, 0:3, :, :], c)
                    nc.scalar.mul(coef[:, 3, :, :], c[:, 2], -1.0).then_inc(s_za, 1)

            def u_high(quad, i):
                b = quad * QI + i
                act.wait_ge(s_u, b + 1)
                if i >= 2 or not isinstance(quad, int) or quad > 0:
                    act.wait_ge(s_E, b - 1)
                nc.scalar.copy(u_parts[i % 2][0][:, :, :], u_spec[i % 2][:, :, :]).then_inc(s_u_hi, 1)

            def mixed(quad, i):
                b = quad * QI + i
                act.wait_ge(s_E, b + 1)
                if i >= 2 or not isinstance(quad, int) or quad > 0:
                    act.wait_ge(s_D, b - 1)
                nc.scalar.copy(mix_parts[i % 2][0][0:CH, :, :], two_halves(P[2], CH, TOK)).then_inc(s_mix, 1)

            def xn_evac(quad, i):
                act.wait_ge(s_X, quad * QI + i + 1)
                nc.scalar.copy(xn_t[i % 2][:, :, :], two_halves(F[i % 2], CH, TOK)).then_inc(s_xnt, 1)

            def logits_copy(quad):
                act.wait_ge(s_L, quad + 1)
                nc.scalar.copy(lg[:, :], P[3][:, 0:TOK]).then_inc(s_la, 1)

            def dispatch_exp(quad):
                act.wait_ge(s_lmax, quad + 1)
                nc.scalar.activation(d_e[:, :], P[3][:, 0:TOK], ACT.Exp, bias=d_m[:, 0:1],
                                     accum_out=d_m[:, 1:2]).then_inc(s_la, 1)

            def dispatch_evac(quad):
                act.wait_ge(s_DT, quad + 1)
                nc.scalar.copy(d_t[:, :, :], two_halves(F[1], HALF, 128)).then_inc(s_dt, 1)

            def combine_exp(quad):
                act.wait_ge(s_csub, quad + 1)
                nc.scalar.activation(c_e[:, :, :], c_s[:, :, :], ACT.Exp).then_inc(s_cexp, 1)

            def combine_evac(quad):
                act.wait_ge(s_CT, quad + 1)
                nc.scalar.copy(c_t[:, :, :], two_halves(F[0], 128, HALF)).then_inc(s_ct, 1)

            def slots_evac(quad):
                act.wait_ge(s_XST, quad + 1)
                nc.scalar.copy(xs_t[:, :, :, :, :].rearrange("p s b n m -> p s (b n m)"),
                               two_halves(P[3], CH, 128)).then_inc(s_xst, 1)

            def gelu(quad):
                act.wait_ge(s_DN, quad + 1)
                for i in range(2):
                    last = nc.scalar.activation(hid[:, i, :], F[1][:, i * QI * NP:(i + 1) * QI * NP], ACT.Gelu,
                                                bias=b_dn[:, i:i + 1])
                last.then_inc(s_gelu, 1)

            def y_evac(quad):
                act.wait_ge(s_UP, quad + 1)
                for b in range(QI):
                    at = slice(32 * b, 32 * b + 32)
                    last = nc.scalar.copy(y_blk[at, b, :], F[1][at, 0:DIM])
                last.then_inc(s_yb, 1)

            def step(g, q, tok, att=True, ffn=True, early=0):
                quad, behind = 2 * g + q, 2 * g + q - 1

                def done(slot):
                    return slot < early

                def embed(slot, halves=(0, 1), early=False):
                    j = (0, 9)[q] + slot
                    if done(slot) and not early:
                        return
                    if tok and j < GRID:
                        x_evac(g + 1, j, halves)
                        if j + 2 < J_ACT and 1 in halves:
                            patches(g + 1, j + 2)

                def at(f, *a):
                    if att:
                        f(quad, *a)

                def ex(f, *a):
                    if ffn:
                        f(behind, *a)

                if q == 0 and tok:
                    patches(g + 1, 0)
                    patches(g + 1, 1)
                for slot in range(early):
                    embed(slot, early=True)
                at(spectra, 0)
                at(spectra, 1)
                embed(0, (0,))
                at(spectra, 2)
                embed(0, (1,))
                at(spectra, 3)
                embed(1)
                at(head_step, 0)
                ex(xn_evac, 0)
                ex(xn_evac, 1)
                embed(2, (0,))
                ex(xn_evac, 2)
                embed(2, (1,))
                ex(xn_evac, 3)
                at(head_step, 1)
                ex(logits_copy)
                embed(3)
                ex(dispatch_exp)
                at(head_step, 2)
                embed(4)
                ex(combine_exp)
                ex(dispatch_evac)
                at(head_step, 3)
                embed(5)
                at(head_step, 4)
                ex(combine_evac)
                ex(slots_evac)
                ex(gelu)
                embed(6, (0,))
                at(u_high, 0)
                embed(6, (1,))
                at(u_high, 1)
                at(mixed, 0)
                ex(y_evac)
                at(u_high, 2)
                at(mixed, 1)
                if q == 0:
                    embed(7)
                at(mixed, 2)
                at(u_high, 3)
                if q == 0:
                    embed(8)
                at(mixed, 3)

            for j in range(2):
                patches(0, j)
            for j in range(GRID):
                x_evac(0, j, start=True)
                if j + 2 < J_ACT:
                    patches(0, j + 2)
            act.wait_ge(s_const, N_CONST)
            step(0, 0, True, ffn=False, early=5)
            step(0, 1, True)
            with act.Fori(1, GROUPS - 1) as g:
                step(g, 0, True)
                step(g, 1, True)
            step(GROUPS - 1, 0, False)
            step(GROUPS - 1, 1, False)
            step(GROUPS, 0, False, att=False)

        @block.vector
        def _(dve):
            LINKS = {"norm": (s_vn, 3), "heads": (s_vh, 1), "experts": (s_vf, 11)}
            linked = {}

            def link(ins, quad, part):
                own, each = LINKS[part]
                linked[part] = linked.get(part, 0) % each + 1
                ins.then_inc(own, 1)
                dve.wait_ge(own, quad * each + linked[part])

            def patches(g, j):
                n = g * GRID + j
                s, w = j // 7, j % 7
                if j in (J_ACT, 7):
                    dve.wait_ge(s_x[s], 16 * g + 16)
                dve.wait_ge(s_tr, 2 * n - 2)
                nc.vector.tensor_copy(x_pat[j % 2][:, :].rearrange("p (r c) -> p r c", r=PATCH),
                                      x_raw[s][:, :, w * PIX:(w + 1) * PIX]).then_inc(s_pat_v, 1)

            def rows(g, j, start=False):
                dve.wait_ge(s_tok, g * GRID + j + 1)
                if j == 0 and (not isinstance(g, int) or g > 1):
                    dve.wait_ge(s_h[0], 128 * g)
                    dve.wait_ge(s_h[1], 128 * g)
                src = (HB, F[1])[j % 2] if start else HB
                dst = first_rows if start else h_rows
                nc.vector.tensor_tensor(dst[:, j, :], src[0:GROWS, 0:DIM], b_tok[:, :],
                                        ALU.add).then_inc(s_rows, 1)

            def moments(stats, m, quad, part):
                me, mo = stats[:, :, :, 1], stats[:, :, :, 4]
                nc.vector.tensor_tensor(m[:, 0, :, :], me, mo, ALU.add)
                nc.vector.tensor_tensor(m[:, 4, :, :], me, mo, ALU.subtract)
                link(nc.vector.tensor_tensor(m[:, 2, :, :], stats[:, :, :, 2], stats[:, :, :, 5], ALU.add), quad, part)
                nc.vector.tensor_scalar(m[:, 0, :, :], m[:, 0, :, :], 0.5, None, ALU.mult)
                nc.vector.tensor_scalar(m[:, 2, :, :], m[:, 2, :, :], 1.0 / DIM, None, ALU.mult)
                link(nc.vector.scalar_tensor_tensor(m[:, 4, :, :], m[:, 4, :, :], 0.25,
                                                    m[:, 4, :, :], ALU.mult, ALU.mult), quad, part)

            def norm_stats(g, q, images=range(QI)):
                quad = 2 * g + q
                if 0 in images:
                    dve.wait_ge(s_h[q], 128 * g + 128)
                for i in images:
                    for c in range(2):
                        last = nc.vector.bn_stats(st[:, c, i, :], h[:, c, q * QI + i, :])
                if QI - 1 not in images:
                    return
                link(last, quad, "norm")
                moments(st, sm, quad, "norm")
                nc.vector.scalar_tensor_tensor(sm[:, 3, :, :], sm[:, 2, :, :], LN_EPS, sm[:, 4, :, :],
                                               ALU.add, ALU.add).then_inc(s_var, 1)

            def norm(g, q, i):
                quad = 2 * g + q
                if i == 0:
                    dve.wait_ge(s_rstd, quad + 1)
                if not isinstance(quad, int) or quad > 0:
                    dve.wait_ge(s_sd, quad * QI + i - 3)
                for c in range(2):
                    last = nc.vector.tensor_scalar(xln[i][:, c, :], h[:, c, q * QI + i, :], sm[:, 0, c, i:i + 1],
                                                   sm[:, 1, c, i:i + 1], ALU.subtract, ALU.mult)
                last.then_inc(s_xln, 1)

            def head_max(quad):
                dve.wait_ge(s_zp, quad * 5 + 3)
                nc.vector.tensor_reduce(z_m[:, 0:1], P[0][:, 0:TOK], AX.X, ALU.max, negate=True).then_inc(s_zv, 1)

            def head_norm(quad):
                dve.wait_ge(s_za, quad * 5 + 3)
                link(nc.vector.reciprocal(z_m[:, 2:3], z_m[:, 1:2]), quad, "heads")
                nc.vector.tensor_scalar(z_n[:, :], z_e[:, :], z_m[:, 2:3], None, ALU.mult).then_inc(s_zv, 1)

            def products(quad, i):
                b = quad * QI + i
                dve.wait_ge(s_B, b + 1)
                if i >= 2 or not isinstance(quad, int) or quad > 0:
                    dve.wait_ge(s_u, b - 1)
                v = P[i % 2][0:HALF, 0:2 * DIM].rearrange("p (s h d) -> p s h d", s=2, d=HD)
                for dst, c0 in ((v_own, 0), (v_cross, 2)):
                    at = dst[i % 2][:, :, :] if c0 == 0 else dst[i % 2][:, ::-1, :]
                    last = nc.vector.tensor_tensor(at.rearrange("p s (h d) -> p s h d", d=HD),
                                                   v, coef_view(coef, c0, i), ALU.mult)
                last.then_inc(s_v, 1)

            def u_low(quad, i):
                dve.wait_ge(s_u_hi, quad * QI + i + 1)
                hi, lo = u_parts[i % 2]
                nc.vector.tensor_tensor(lo[:, :, :], u_spec[i % 2][:, :, :], hi[:, :, :].bitcast(F32),
                                        ALU.subtract).then_inc(s_u_lo, 1)

            def mixed_low(quad, i):
                dve.wait_ge(s_mix, quad * QI + i + 1)
                hi, lo = mix_parts[i % 2]
                nc.vector.tensor_tensor(lo[0:CH, :, :], P[2][0:CH, 0:2 * TOK].rearrange("p (c k) -> p c k", c=2),
                                        hi[0:CH, :, :].bitcast(F32), ALU.subtract).then_inc(s_mix_lo, 1)

            def residual(quad, i, q):
                b = quad * QI + i
                dve.wait_ge(s_D, b + 1)
                nc.vector.tensor_tensor(h1[:, :, q * QI + i, :],
                                        P[3][0:HALF, 0:2 * DIM].rearrange("p (c d) -> p c d", c=2),
                                        h[:, :, q * QI + i, :], ALU.add).then_inc(s_h1, 1)
                dve.wait_ge(s_h1, b + 1)
                for c in range(2):
                    last = nc.vector.bn_stats(st2[:, c, i, :], h1[:, c, q * QI + i, :])
                if i == QI - 1:
                    link(last, quad, "experts")
                    moments(st2, sm2, quad, "experts")
                    link(nc.vector.tensor_tensor(sm2[:, 2, :, :], sm2[:, 2, :, :], sm2[:, 4, :, :], ALU.add),
                         quad, "experts")
                    nc.vector.tensor_scalar(sm2[:, 3, :, :], sm2[:, 2, :, :], LN_EPS, None, ALU.add)
                    nc.vector.tensor_scalar(sm2[:, 2, :, :], sm2[:, 2, :, :], float(DIM), None,
                                            ALU.mult).then_inc(s_var2, 1)

            def unit_scale(quad):
                dve.wait_ge(s_root, quad + 1)
                link(nc.vector.scalar_tensor_tensor(sm2[:, 7, :, :], sm2[:, 6, :, :], L2_EPS,
                                                    sm2[:, 5, :, :], ALU.mult, ALU.add), quad, "experts")
                link(nc.vector.reciprocal(sm2[:, 1, :, :], sm2[:, 7, :, :]), quad, "experts")

            def unit(quad, i, q):
                for c in range(2):
                    last = nc.vector.tensor_scalar(xn[:, i, c, :], h1[:, c, q * QI + i, :], sm2[:, 0, c, i:i + 1],
                                                   sm2[:, 1, c, i:i + 1], ALU.subtract, ALU.mult)
                last.then_inc(s_xn, 1)

            def slot_max(quad):
                dve.wait_ge(s_L, quad + 1)
                dve.wait_ge(s_la, quad * 2 + 1)
                nc.vector.tensor_reduce(d_m[:, 0:1], P[3][:, 0:TOK], AX.X, ALU.max, negate=True).then_inc(s_lmax, 1)

            def slot_recip(quad):
                dve.wait_ge(s_la, quad * 2 + 2)
                link(nc.vector.reciprocal(d_m[:, 2:3], d_m[:, 1:2]), quad, "experts")

            def combine_sub(quad):
                dve.wait_ge(s_LT, quad + 1)
                l_t = F[0][0:HALF, 0:256].rearrange("p (k s) -> p k s", s=SLOTS)
                link(nc.vector.tensor_reduce(c_m[:, 0, :], l_t, AX.X, ALU.max), quad, "experts")
                nc.vector.tensor_tensor(c_s[:, :, :], l_t, spread(c_m[:, 0, :]), ALU.subtract).then_inc(s_csub, 1)

            def combine_norm(quad):
                dve.wait_ge(s_cexp, quad + 1)
                link(nc.vector.tensor_reduce(c_m[:, 1, :], c_e[:, :, :], AX.X, ALU.add), quad, "experts")
                link(nc.vector.reciprocal(c_m[:, 2, :], c_m[:, 1, :]), quad, "experts")
                nc.vector.tensor_tensor(c_n[:, :, :], c_e[:, :, :], spread(c_m[:, 2, :]), ALU.mult).then_inc(s_cn, 1)

            def slot_inputs(quad):
                dve.wait_ge(s_XS, quad + 1)
                nc.vector.tensor_scalar(xs[:, :], P[2][:, 0:DIM], d_m[:, 2:3], None, ALU.mult).then_inc(s_xs, 1)

            def hidden_blocks(quad):
                dve.wait_ge(s_gelu, quad + 1)
                link(nc.vector.tensor_scalar(hid1[:, :, :], hid[:, :, :], one[:, 0:1], None, ALU.add), quad, "experts")
                for i in range(2):
                    last = nc.vector.tensor_tensor(hid_blk[:, i], over_experts(hid1[:, i, :]),
                                                   over_images(mask[:, i, :]), ALU.mult)
                last.then_inc(s_blk, 1)

            def output(quad, u, q):
                c, pair = u // 2, u % 2
                if u == 0 and (not isinstance(quad, int) or quad >= 2):
                    dve.wait_ge(s_out[q], 16 * (quad + 1 - q))
                dve.wait_ge(s_Y, quad * 4 + u + 1)
                b0 = q * QI + 2 * pair
                nc.vector.tensor_tensor(o_sb[q][:, c, 2 * pair:2 * pair + 2, :],
                                        F[u % 2][0:HALF, 0:2 * DIM].rearrange("p (b d) -> p b d", b=2),
                                        h1[:, c, b0:b0 + 2, :], ALU.add).then_inc(s_o, 1)

            def split_weights():
                dve.wait_ge(s_const, N_CONST)
                dve.wait_ge(s_zero, 1)
                whole = ((w_v, w_v_parts), (w_p, w_p_parts), (inv, inv_parts))
                for w, (hi, _) in whole:
                    nc.vector.tensor_copy(hi[...], w[...]).then_inc(s_parts, 1)
                dve.wait_ge(s_parts, 3)
                for w, (hi, lo) in whole:
                    nc.vector.tensor_tensor(lo[...], w[...], hi[...].bitcast(F32), ALU.subtract).then_inc(s_parts, 1)

            def scale_slots():
                dve.wait_ge(s_const, N_CONST)
                nc.vector.tensor_tensor(slots_sq[:, :, :], slots[:, :, :], slots[:, :, :], ALU.mult).then_inc(s_ready, 1)
                dve.wait_ge(s_ready, 1)
                nc.vector.tensor_reduce(slot_norm[:, 0], slots_sq[:, :, :].rearrange("p s (n m) -> p s m n", m=NP),
                                        AX.X, ALU.add).then_inc(s_ready, 1)
                dve.wait_ge(s_ready, 3)
                nc.vector.tensor_scalar(slot_norm[:, 2], slot_norm[:, 1], L2_EPS, None, ALU.add).then_inc(s_ready, 1)
                dve.wait_ge(s_ready, 4)
                nc.vector.reciprocal(slot_norm[:, 3], slot_norm[:, 2]).then_inc(s_ready, 1)
                dve.wait_ge(s_ready, 5)
                nc.vector.tensor_scalar(slot_norm[:, 0], slot_norm[:, 3], scale_c[:, 0:1], None,
                                        ALU.mult).then_inc(s_ready, 1)
                dve.wait_ge(s_ready, 6)
                for s in range(2):
                    last = nc.vector.tensor_tensor(slots_n[:, s, :].rearrange("p (n m) -> p n m", m=NP),
                                                   slots[:, s, :].rearrange("p (n m) -> p n m", m=NP),
                                                   slot_norm[:, 0, s, :].unsqueeze(1).to_broadcast([CH, NE, NP]), ALU.mult)
                last.then_inc(s_ready, 1)

            def step(g, q, tok, att=True, ffn=True, early=0):
                quad, behind = 2 * g + q, 2 * g + q - 1

                def done(slot):
                    return slot < early

                def embed(slot, early=False):
                    j = (0, 9)[q] + slot
                    if done(slot) and not early:
                        return
                    if tok and J_ACT <= j + 2 < GRID:
                        patches(g + 1, j + 2)
                    if tok and 1 <= j <= GRID:
                        rows(g + 1, j - 1)

                def at(f, *a):
                    if att:
                        f(quad, *a)

                def ex(f, *a):
                    if ffn:
                        f(behind, *a)

                def ahead(f, *a):
                    if q == 0 and att:
                        f(g, 1, *a)
                    elif tok:
                        f(g + 1, 0, *a)
                if early:
                    embed(0, early=True)
                    embed(1, early=True)
                    embed(2, early=True)
                    norm_stats(0, 0)
                    for i in range(QI):
                        norm(0, 0, i)
                    for slot in range(3, early):
                        embed(slot, early=True)
                if early:
                    scale_slots()
                    split_weights()
                embed(0)
                ex(unit_scale)
                ex(unit, 0, 1 - q)
                ex(unit, 1, 1 - q)
                embed(1)
                ex(unit, 2, 1 - q)
                ex(unit, 3, 1 - q)
                embed(2)
                if q == 0:
                    ahead(norm_stats)
                ex(slot_max)
                embed(3)
                at(head_max)
                at(head_norm)
                ex(combine_sub)
                ex(slot_recip)
                embed(4)
                ex(combine_norm)
                ex(slot_inputs)
                embed(5)
                if q == 0:
                    for i in range(QI):
                        ahead(norm, i)
                at(products, 0)
                at(products, 1)
                ex(hidden_blocks)
                at(u_low, 0)
                embed(6)
                at(u_low, 1)
                at(products, 2)
                at(mixed_low, 0)
                if q == 1:
                    ahead(norm_stats, range(0, 2))
                at(u_low, 2)
                at(products, 3)
                at(mixed_low, 1)
                at(residual, 0, q)
                if q == 1:
                    ahead(norm_stats, range(2, 4))
                if q == 0:
                    embed(7)
                at(u_low, 3)
                at(mixed_low, 2)
                ex(output, 0, 1 - q)
                at(residual, 1, q)
                ex(output, 1, 1 - q)
                if q == 0:
                    embed(8)
                if q == 1:
                    ahead(norm, 0)
                    ahead(norm, 1)
                at(mixed_low, 3)
                at(residual, 2, q)
                if q == 1:
                    ahead(norm, 2)
                ex(output, 2, 1 - q)
                ex(output, 3, 1 - q)
                if q == 1:
                    ahead(norm, 3)
                at(residual, 3, q)
            dve.wait_ge(s_embed, 48)
            for j in range(GRID):
                if J_ACT <= j + 2 < GRID:
                    patches(0, j + 2)
                rows(0, j, start=True)

            step(0, 0, True, ffn=False, early=5)
            step(0, 1, True)
            with dve.Fori(1, GROUPS - 1) as g:
                step(g, 0, True)
                step(g, 1, True)
            step(GROUPS - 1, 0, False)
            step(GROUPS - 1, 1, False)
            step(GROUPS, 0, False, att=False)

        @block.tensor
        def _(pe):
            def mm(dst, lhsT, rhs, start=True, stop=True, **kw):
                return nc.tensor.matmul(dst, lhsT, rhs, start=start, stop=stop, **kw)

            def mm_parts(dst, lhs, rhs, start=True, stop=True):
                mm(dst, lhs[0], rhs[0], start=start, stop=False)
                mm(dst, lhs[0], rhs[1], start=False, stop=False)
                return mm(dst, lhs[1], rhs[0], start=False, stop=stop)

            def turn_x(g, j, i, start=False):
                n = g * GRID + j
                if i == 0 and j < J_ACT:
                    pe.wait_ge(s_pat_a, g * J_ACT + j + 1)
                elif i == 0:
                    pe.wait_ge(s_pat_v, g * J_VEC + j - J_ACT + 1)
                if start and j >= 1:
                    pe.wait_ge(s_xt, 2 * n - 1 + i)
                elif not start:
                    pe.wait_ge(s_xt, 2 * n + i)
                dst = (TR, F[0])[i] if start else TR
                for q in range(3):
                    k = 3 * i + q
                    last = nc.tensor.transpose(dst[:, q * GROWS:(q + 1) * GROWS],
                                               x_pat[j % 2][:, k * 128:(k + 1) * 128], ident[0:GROWS, 0:GROWS])
                last.then_inc(s_tr, 1)

            def embed_x(g, j, i, start=False):
                n = g * GRID + j
                if i == 0 and (j >= 2 or not start):
                    pe.wait_ge(s_rows, n - 1 if start else n)
                pe.wait_ge(s_xt, 2 * n + 1 + i)
                dst = (HB, F[1])[j % 2] if start else HB
                for k in range(3 * i, 3 * i + 3):
                    last = mm(dst[0:GROWS, 0:DIM], x_t[j % 2][:, k, :], w_tok[:, k, :],
                              start=(k == 0), stop=(k == KQ - 1))
                if i == 1:
                    last.then_inc(s_tok, 1)

            def forward(quad, i):
                pe.wait_ge(s_sd, quad * QI + i + 1)
                if i >= 2:
                    pe.wait_ge(s_spec, quad * QI + i - 1)
                dst = P[i % 2][0:CH, 0:2 * TOK].rearrange("p (s c k) -> p s c k", s=2, c=2)
                for s in range(2):
                    for e in range(2):
                        last = mm(dst[:, s, :, e * QTR:(e + 1) * QTR], sumdif[i][:, e, s * CH:(s + 1) * CH],
                                  fwd[:, e, :])
                last.then_inc(s_A, 1)

            def head_step(quad, k):
                if k == 0:
                    pe.wait_ge(s_spec, quad * QI + QI)
                    for i in range(QI):
                        for s in range(2):
                            last = mm(P[0][32 * i:32 * i + 32, 0:TOK], w_a[:, s, :], spec[i][:, s, :],
                                      start=(s == 0), stop=(s == 1))
                elif k == 1:
                    pe.wait_ge(s_za, quad * 5 + 1)
                    for c in range(2):
                        last = nc.tensor.transpose(P[1][0:HALF, c * 128:(c + 1) * 128],
                                                   zh[:, c * HALF:(c + 1) * HALF], ident[:, :])
                elif k == 2:
                    pe.wait_ge(s_za, quad * 5 + 2)
                    for c in range(2):
                        last = mm(P[0][:, 0:TOK], zh_t[:, c, :], inv[:, c, :], start=(c == 0), stop=(c == 1))
                elif k == 3:
                    pe.wait_ge(s_zv, quad * 2 + 2)
                    for c in range(2):
                        last = nc.tensor.transpose(P[1][0:HALF, c * 128:(c + 1) * 128],
                                                   z_n[:, c * HALF:(c + 1) * HALF], ident[:, :])
                else:
                    pe.wait_ge(s_za, quad * 5 + 4)
                    for k in range(3):
                        dst = P[0][0:HALF, k * QI * HEADS:(k + 1) * QI * HEADS].rearrange("p (b h) -> p b h", b=QI)
                        for c in range(2):
                            rows_c = z_t[:, c, :].rearrange("p (b h) -> p b h", b=QI)[:, :, 0:HEADS]
                            last = mm(dst, headb[:, c, k, :], rows_c, start=(c == 0), stop=(c == 1))
                last.then_inc(s_zp, 1)

            def values(quad, i):
                if i == 0:
                    pe.wait_ge(s_za, quad * 5 + 5)
                    pe.wait_ge(s_parts, 6)
                elif i >= 2:
                    pe.wait_ge(s_v, quad * QI + i - 1)
                pe.wait_ge(s_spec_lo, quad * QI + i + 1)
                for c in range(2):
                    for s in range(2):
                        last = mm_parts(P[i % 2][0:HALF, c * DIM:(c + 1) * DIM],
                                        [part[:, s, c * HALF:(c + 1) * HALF] for part in spec_parts[i]],
                                        [part[:, s, :] for part in w_v_parts], start=(s == 0), stop=(s == 1))
                last.then_inc(s_B, 1)

            def inverse(quad, i):
                b = quad * QI + i
                pe.wait_ge(s_u_lo, b + 1)
                if i >= 1 or not isinstance(quad, int) or quad > 0:
                    pe.wait_ge(s_mix_lo, b)
                for s in range(2):
                    for c in range(2):
                        last = mm_parts(P[2][0:CH, s * TOK:(s + 1) * TOK],
                                        [part[:, c, s * CH:(s + 1) * CH] for part in u_parts[i % 2]],
                                        [part[:, c, :] for part in inv_parts], start=(c == 0), stop=(c == 1))
                last.then_inc(s_E, 1)

            def project(quad, i):
                b = quad * QI + i
                pe.wait_ge(s_mix_lo, b + 1)
                if i >= 1 or not isinstance(quad, int) or quad > 0:
                    pe.wait_ge(s_h1, b)
                for c in range(2):
                    tk = slice(c * HALF, (c + 1) * HALF)
                    dst, (hi, lo), (w_hi, w_lo) = P[3][0:HALF, c * DIM:(c + 1) * DIM], mix_parts[i % 2], w_p_parts
                    mm_parts(dst, (hi[0:CH, 0, tk], lo[0:CH, 0, tk]), (w_hi[0:CH, 0, :], w_lo[0:CH, 0, :]), stop=False)
                    mm(dst, hi[:, 1, tk], w_hi[:, 1, :], start=False, stop=False)
                    mm(dst, hi[:, 1, tk], w_lo[:, 1, :], start=False, stop=False)
                    last = mm(dst, lo[0:CH, 1, tk], w_hi[0:CH, 1, :], start=False)
                last.then_inc(s_D, 1)

            def turn_units(quad, i):
                pe.wait_ge(s_xn, quad * QI + i + 1)
                if i >= 2:
                    pe.wait_ge(s_xnt, quad * QI + i - 1)
                elif not isinstance(quad, int) or quad > 0:
                    pe.wait_ge(s_o, quad * 4)
                for s in range(2):
                    for c in range(2):
                        at = s * TOK + c * HALF
                        last = nc.tensor.transpose(F[i % 2][0:CH, at:at + HALF], xn[:, i, c, s * CH:(s + 1) * CH],
                                                   ident[0:HALF, 0:HALF])
                last.then_inc(s_X, 1)

            def logits(quad, i):
                pe.wait_ge(s_xnt, quad * QI + i + 1)
                for s in range(2):
                    last = mm(P[3][32 * i:32 * i + 32, 0:TOK], slots_n[:, s, :], xn_t[i % 2][:, s, :],
                              start=(s == 0), stop=(s == 1))
                if i == QI - 1:
                    last.then_inc(s_L, 1)

            def turn_logits(quad):
                pe.wait_ge(s_la, quad * 2 + 1)
                for c in range(2):
                    last = nc.tensor.transpose(F[0][0:HALF, c * 128:(c + 1) * 128],
                                               lg[:, c * HALF:(c + 1) * HALF], ident[:, :])
                last.then_inc(s_LT, 1)

            def turn_dispatch(quad):
                pe.wait_ge(s_la, quad * 2 + 2)
                for c in range(2):
                    last = nc.tensor.transpose(F[1][0:HALF, c * 128:(c + 1) * 128],
                                               d_e[:, c * HALF:(c + 1) * HALF], ident[:, :])
                last.then_inc(s_DT, 1)

            def slot_inputs(quad):
                pe.wait_ge(s_dt, quad + 1)
                for i in range(QI):
                    for c in range(2):
                        last = mm(P[2][32 * i:32 * i + 32, 0:DIM], d_t[:, c, 32 * i:32 * i + 32],
                                  xn[:, i, c, :], start=(c == 0), stop=(c == 1))
                last.then_inc(s_XS, 1)

            def turn_slots(quad):
                pe.wait_ge(s_xs, quad + 1)
                for s in range(2):
                    last = nc.tensor.transpose(P[3][0:CH, s * 128:(s + 1) * 128],
                                               xs[:, s * CH:(s + 1) * CH], ident[:, :])
                last.then_inc(s_XST, 1)

            def turn_combine(quad):
                pe.wait_ge(s_cn, quad + 1)
                for c in range(2):
                    last = nc.tensor.transpose(F[0][:, c * HALF:(c + 1) * HALF],
                                               c_n[:, c * QI:(c + 1) * QI, :].rearrange("p b s -> p (b s)"),
                                               ident[0:HALF, 0:HALF])
                last.then_inc(s_CT, 1)

            def expert_down(quad):
                pe.wait_ge(s_xst, quad + 1)
                for n in range(NE):
                    i = n // 4
                    for s in range(2):
                        last = mm(F[1][32 * (n % 4):32 * (n % 4) + 32, QI * NP * i:QI * NP * (i + 1)].rearrange(
                            "p (b m) -> p b m", m=NP), w_dn[:, s, n, :], xs_t[:, s, :, n, :],
                            start=(s == 0), stop=(s == 1))
                last.then_inc(s_DN, 1)

            def expert_up(quad):
                pe.wait_ge(s_blk, quad + 1)
                for i in range(2):
                    last = mm(F[1][:, 0:DIM], hid_blk[:, i].rearrange("p b n m -> p (b n m)"),
                              w_up[:, i, :], start=(i == 0), stop=(i == 1))
                last.then_inc(s_UP, 1)

            def combine(quad, u):
                c, pair = u // 2, u % 2
                if u == 0:
                    pe.wait_ge(s_ct, quad + 1)
                    pe.wait_ge(s_yb, quad + 1)
                if u >= 2:
                    pe.wait_ge(s_o, quad * 4 + u - 1)
                mm(F[u % 2][0:HALF, 0:2 * DIM], c_t[:, c, :],
                   y_blk[:, 2 * pair:2 * pair + 2, :].rearrange("p b d -> p (b d)")).then_inc(s_Y, 1)

            def step(g, q, tok, att=True, ffn=True, early=0):
                quad, behind = 2 * g + q, 2 * g + q - 1

                def done(slot):
                    return slot < early

                def embed(slot, halves=(0, 1), early=False):
                    j = (0, 9)[q] + slot
                    for i in halves if early or not done(slot) else ():
                        if tok and j < GRID:
                            turn_x(g + 1, j, i)
                        if tok and 1 <= j <= GRID:
                            embed_x(g + 1, j - 1, i)

                def at(f, *a):
                    if att:
                        f(quad, *a)

                def ex(f, *a):
                    if ffn:
                        f(behind, *a)
                for slot in range(early):
                    embed(slot, early=True)
                if early:
                    pe.wait_ge(s_const, N_CONST)
                    pe.wait_ge(s_zero, 1)
                at(forward, 0)
                at(forward, 1)
                embed(0, (0,))
                at(forward, 2)
                embed(0, (1,))
                at(forward, 3)
                embed(1)
                at(head_step, 0)
                ex(turn_units, 0)
                ex(turn_units, 1)
                embed(2, (0,))
                ex(logits, 0)
                ex(turn_units, 2)
                ex(logits, 1)
                embed(2, (1,))
                ex(turn_units, 3)
                ex(logits, 2)
                at(head_step, 1)
                ex(logits, 3)
                embed(3)
                at(head_step, 2)
                ex(turn_logits)
                embed(4)
                ex(turn_dispatch)
                at(head_step, 3)
                embed(5, (0,))
                ex(slot_inputs)
                embed(5, (1,))
                at(head_step, 4)
                ex(turn_combine)
                at(values, 0)
                ex(turn_slots)
                at(values, 1)
                ex(expert_down)
                at(values, 2)
                embed(6)
                at(inverse, 0)
                ex(expert_up)
                at(values, 3)
                at(inverse, 1)
                at(project, 0)
                ex(combine, 0)
                if q == 0:
                    embed(7)
                at(inverse, 2)
                at(project, 1)
                ex(combine, 1)
                if q == 0:
                    embed(8)
                at(inverse, 3)
                at(project, 2)
                ex(combine, 2)
                ex(combine, 3)
                at(project, 3)

            pe.wait_ge(s_embed, 48)
            for i in range(2):
                turn_x(0, 0, i, start=True)
            for j in range(GRID):
                for i in range(2):
                    if j + 1 < GRID:
                        turn_x(0, j + 1, i, start=True)
                for i in range(2):
                    embed_x(0, j, i, start=True)
            step(0, 0, True, ffn=False, early=5)
            pe.wait_ge(s_ready, 7)
            pe.wait_ge(s_rows, GRID)
            step(0, 1, True)
            with pe.Fori(1, GROUPS - 1) as g:
                step(g, 0, True)
                step(g, 1, True)
            step(GROUPS - 1, 0, False)
            step(GROUPS - 1, 1, False)
            step(GROUPS, 0, False, att=False)


def coef_view(c, first, image):
    v = c[:, first:first + 2, image, :]
    return v.unsqueeze(3).to_broadcast([HALF, 2, HEADS, HD])


def spread(v):
    return v.unsqueeze(2).to_broadcast([HALF, 2 * QI, SLOTS])


def over_experts(v):
    return v.rearrange("p (b o m) -> p b o m", o=1, m=NP).to_broadcast([128, QI, NE, NP])


def over_images(v):
    return v.rearrange("p (o n m) -> p o n m", o=1, m=NP).to_broadcast([128, QI, NE, NP])


_INS = ["x", "L0_tok_W", "L0_tok_b", "L0_attn_W_A", "L0_attn_W_V", "L0_attn_W_proj", "L0_attn_b_proj",
        "L0_ffn_slot_params", "L0_ffn_scale", "L0_ffn_W_down", "L0_ffn_b_down", "L0_ffn_W_up", "L0_ffn_b_up"]


def kernel(**inputs):
    import concourse.bacc as bacc
    from concourse.bass_utils import run_bass_kernel_spmd

    nc = bacc.Bacc("TRN2", target_bir_lowering=False, num_devices=1)
    arrays, args = {}, []
    for name in _INS:
        a = np.ascontiguousarray(inputs[name])
        if a.ndim == 0 or name == "L0_ffn_scale":
            a = a.reshape(1, 1)
        arrays[f"in_{name}"] = a
    for name, a in tables().items():
        arrays[f"table_{name}"] = a
    for name, a in arrays.items():
        args.append(nc.dram_tensor(name, a.shape, mybir.dt.from_np(a.dtype), kind="ExternalInput").ap())
    args.append(nc.dram_tensor("out", (IMAGES, TOK, DIM), F32, kind="ExternalOutput").ap())
    build(nc, *args)
    r = run_bass_kernel_spmd(nc, [arrays], core_ids=[0])
    return r.results[0]["out"]
```
